# Optimizing a Trainium2 kernel written in Bass

```python
import numpy as np
import jax
import jax.numpy as jnp

def _softmax(x, axis=-1):
    return jax.nn.softmax(x, axis=axis)

def _gelu(x):
    return jax.nn.gelu(x, approximate=True)

def _silu(x):
    return jax.nn.silu(x)

def _sigmoid(x):
    return jax.nn.sigmoid(x)

def _layernorm(x, axis=-1, eps=1e-05):
    m = jnp.mean(x, axis=axis, keepdims=True)
    v = jnp.var(x, axis=axis, keepdims=True)
    return (x - m) / jnp.sqrt(v + eps)

def _scatter_add(tgt, idx, src, axis=0):
    return tgt.at[idx].add(src)

def _segment_sum(src, seg, n):
    return jax.ops.segment_sum(src, seg, n)
kernel_name = 'mk_prb_d1_jaxref_r4_6cadab'

def setup_inputs(seed: int=0):
    np.random.seed(seed)
    _w = jnp.asarray

    def _L0_attn_setup():
        import jax, jax.numpy as jnp
        import numpy as np
        HIDDEN = 512
        N_HEAD = 16
        N_KV_HEAD = 8
        Q_LORA = 192
        KV_LORA = 128
        ROPE_DIM = 64
        NOPE_DIM = 128
        V_DIM = 128
        ROPE_BASE = 10000.0
        EPS = 1e-06
        SCALE = (NOPE_DIM + ROPE_DIM) ** (-0.5)

        def rms_norm(x, w):
            var = jnp.mean(jnp.square(x), axis=-1, keepdims=True)
            return x * jax.lax.rsqrt(var + EPS) * w

        def rotate_half(x):
            x1, x2 = jnp.split(x, 2, axis=-1)
            return jnp.concatenate([-x2, x1], axis=-1)

        def rope_cos_sin(seq_len, dtype=jnp.float32):
            inv_freq = 1.0 / ROPE_BASE ** (jnp.arange(0, ROPE_DIM, 2, dtype=jnp.float32) / ROPE_DIM)
            pos = jnp.arange(seq_len, dtype=jnp.float32)
            freqs = jnp.outer(pos, inv_freq)
            emb = jnp.concatenate([freqs, freqs], axis=-1)
            return (jnp.cos(emb).astype(dtype), jnp.sin(emb).astype(dtype))
        key = jax.random.key(seed)
        ks = jax.random.split(key, 12)
        B, T = (2, 512)

        def w(k, shape):
            fan_in = shape[0]
            return jax.random.normal(k, shape, dtype=jnp.float32) * (1.0 / np.sqrt(fan_in))
        return {'x': jax.random.normal(ks[0], (B, T, HIDDEN), dtype=jnp.float32), 'Wq_down': w(ks[1], (HIDDEN, Q_LORA)), 'q_norm_w': jnp.ones((Q_LORA,), jnp.float32), 'Wq_up': w(ks[2], (Q_LORA, N_HEAD * NOPE_DIM)), 'Wq_pe': w(ks[3], (Q_LORA, N_HEAD * ROPE_DIM)), 'Wkv_down': w(ks[4], (HIDDEN, KV_LORA)), 'kv_norm_w': jnp.ones((KV_LORA,), jnp.float32), 'Wkv_up': w(ks[5], (KV_LORA, N_KV_HEAD * (V_DIM + V_DIM))), 'Wk_pe': w(ks[6], (HIDDEN, ROPE_DIM)), 'k_pe_norm_w': jnp.ones((ROPE_DIM,), jnp.float32), 'Wo': w(ks[7], (N_HEAD * V_DIM, HIDDEN))}
    _L0_attn_in = _L0_attn_setup()

    def _L0_ffn_setup():
        import jax, jax.numpy as jnp
        import numpy as np

        def ternary_quantize(t, threshold, scale):
            return jnp.where(t > threshold, scale, jnp.where(t < -threshold, -scale, 0.0)).astype(t.dtype)
        key = jax.random.key(seed)
        k1, k2, k3 = jax.random.split(key, 3)
        B, S, D = (4, 1024, 512)
        x = jax.random.normal(k1, (B, S, D), dtype=jnp.float32)
        weight = jax.random.normal(k2, (D, D), dtype=jnp.float32) * 0.02
        rram_variation = jax.random.normal(k3, (D, D), dtype=jnp.float32) * 0.05
        return {'x': x, 'weight': weight, 'rram_variation': rram_variation}
    _L0_ffn_in = _L0_ffn_setup()
    _d = {'L0_attn_x': _L0_attn_in['x'], 'L0_attn_Wq_down': _L0_attn_in['Wq_down'], 'L0_attn_q_norm_w': _L0_attn_in['q_norm_w'], 'L0_attn_Wq_up': _L0_attn_in['Wq_up'], 'L0_attn_Wq_pe': _L0_attn_in['Wq_pe'], 'L0_attn_Wkv_down': _L0_attn_in['Wkv_down'], 'L0_attn_kv_norm_w': _L0_attn_in['kv_norm_w'], 'L0_attn_Wkv_up': _L0_attn_in['Wkv_up'], 'L0_attn_Wk_pe': _L0_attn_in['Wk_pe'], 'L0_attn_k_pe_norm_w': _L0_attn_in['k_pe_norm_w'], 'L0_attn_Wo': _L0_attn_in['Wo'], 'L0_ffn_weight': _L0_ffn_in['weight'], 'L0_ffn_rram_variation': _L0_ffn_in['rram_variation']}
    _x0 = _d['L0_attn_x']
    _d['L0_attn_x'] = jax.random.normal(jax.random.fold_in(jax.random.key(seed), 1), (4, 1024, 512), dtype=_x0.dtype)
    del _x0
    return _d

def reference(L0_attn_x, L0_attn_Wq_down, L0_attn_q_norm_w, L0_attn_Wq_up, L0_attn_Wq_pe, L0_attn_Wkv_down, L0_attn_kv_norm_w, L0_attn_Wkv_up, L0_attn_Wk_pe, L0_attn_k_pe_norm_w, L0_attn_Wo, L0_ffn_weight, L0_ffn_rram_variation):

    def _L0_attn_ref(x, Wq_down, q_norm_w, Wq_up, Wq_pe, Wkv_down, kv_norm_w, Wkv_up, Wk_pe, k_pe_norm_w, Wo):
        import jax, jax.numpy as jnp
        import numpy as np
        HIDDEN = 512
        N_HEAD = 16
        N_KV_HEAD = 8
        Q_LORA = 192
        KV_LORA = 128
        ROPE_DIM = 64
        NOPE_DIM = 128
        V_DIM = 128
        ROPE_BASE = 10000.0
        EPS = 1e-06
        SCALE = (NOPE_DIM + ROPE_DIM) ** (-0.5)

        def rms_norm(x, w):
            var = jnp.mean(jnp.square(x), axis=-1, keepdims=True)
            return x * jax.lax.rsqrt(var + EPS) * w

        def rotate_half(x):
            x1, x2 = jnp.split(x, 2, axis=-1)
            return jnp.concatenate([-x2, x1], axis=-1)

        def rope_cos_sin(seq_len, dtype=jnp.float32):
            inv_freq = 1.0 / ROPE_BASE ** (jnp.arange(0, ROPE_DIM, 2, dtype=jnp.float32) / ROPE_DIM)
            pos = jnp.arange(seq_len, dtype=jnp.float32)
            freqs = jnp.outer(pos, inv_freq)
            emb = jnp.concatenate([freqs, freqs], axis=-1)
            return (jnp.cos(emb).astype(dtype), jnp.sin(emb).astype(dtype))
        B, T, C = x.shape
        c_Q = rms_norm(x @ Wq_down, q_norm_w)
        q_nop = (c_Q @ Wq_up).reshape(B, T, N_HEAD, NOPE_DIM)
        q_pe = (c_Q @ Wq_pe).reshape(B, T, N_HEAD, ROPE_DIM)
        c_KV = rms_norm(x @ Wkv_down, kv_norm_w)
        kv_up = c_KV @ Wkv_up
        k_nop, v = jnp.split(kv_up, 2, axis=-1)
        k_nop = k_nop.reshape(B, T, N_KV_HEAD, V_DIM)
        v = v.reshape(B, T, N_KV_HEAD, V_DIM)
        group = N_HEAD // N_KV_HEAD
        k_nop = jnp.repeat(k_nop, group, axis=2)
        v = jnp.repeat(v, group, axis=2)
        k_pe = rms_norm(x @ Wk_pe, k_pe_norm_w).reshape(B, T, 1, ROPE_DIM)
        q_nop = q_nop.transpose(0, 2, 1, 3)
        q_pe = q_pe.transpose(0, 2, 1, 3)
        k_nop = k_nop.transpose(0, 2, 1, 3)
        k_pe = k_pe.transpose(0, 2, 1, 3)
        v = v.transpose(0, 2, 1, 3)
        cos, sin = rope_cos_sin(T, x.dtype)
        cos = cos[None, None]
        sin = sin[None, None]
        q_pe = q_pe * cos + rotate_half(q_pe) * sin
        k_pe = k_pe * cos + rotate_half(k_pe) * sin
        k_pe = jnp.broadcast_to(k_pe, (B, N_HEAD, T, ROPE_DIM))
        q = jnp.concatenate([q_nop, q_pe], axis=-1)
        k = jnp.concatenate([k_nop, k_pe], axis=-1)
        scores = jnp.einsum('bhqd,bhkd->bhqk', q, k) * SCALE
        mask = jnp.tril(jnp.ones((T, T), dtype=bool))
        scores = jnp.where(mask[None, None], scores, jnp.finfo(scores.dtype).min)
        attn = jax.nn.softmax(scores, axis=-1)
        y = jnp.einsum('bhqk,bhkd->bhqd', attn, v)
        y = y.transpose(0, 2, 1, 3).reshape(B, T, N_HEAD * V_DIM)
        return y @ Wo

    def _L0_ffn_ref(x, weight, rram_variation):
        import jax, jax.numpy as jnp
        import numpy as np

        def ternary_quantize(t, threshold, scale):
            return jnp.where(t > threshold, scale, jnp.where(t < -threshold, -scale, 0.0)).astype(t.dtype)
        TH_X, SC_X = (0.33, 0.5)
        TH_W, SC_W = (0.2, 0.6)
        x_q = ternary_quantize(x, TH_X, SC_X)
        w_q = ternary_quantize(weight, TH_W, SC_W)
        w_rram = w_q + rram_variation
        return jnp.einsum('bsd,od->bso', x_q, w_rram)
    x = L0_attn_x
    xn = _layernorm(x, axis=-1)
    x = x + _L0_attn_ref(xn, L0_attn_Wq_down, L0_attn_q_norm_w, L0_attn_Wq_up, L0_attn_Wq_pe, L0_attn_Wkv_down, L0_attn_kv_norm_w, L0_attn_Wkv_up, L0_attn_Wk_pe, L0_attn_k_pe_norm_w, L0_attn_Wo) + _L0_ffn_ref(xn, L0_ffn_weight, L0_ffn_rram_variation)
    return x

_drawn_inputs = setup_inputs


def setup_inputs(seed=0):
    import zlib

    import numpy as np

    out = dict(_drawn_inputs(seed))
    spreads = {'L0_attn_q_norm_w': (1.0, 0.556),
     'L0_attn_kv_norm_w': (1.0, 0.2),
     'L0_attn_k_pe_norm_w': (1.0, 0.6)}
    factors = {}
    for name, (base, spread) in spreads.items():
        noise = np.random.default_rng([zlib.crc32(name.encode()), seed]).standard_normal(out[name].shape)
        drawn = base * np.exp(spread * noise) if base else spread * noise
        out[name] = jnp.asarray(drawn.astype(out[name].dtype))
    for name, factor in factors.items():
        out[name] = (out[name] * factor).astype(out[name].dtype)
    return out
```

```python
from contextlib import ExitStack

import numpy as np

import concourse.bass as bass
from concourse import mybir

F32 = mybir.dt.float32
F32R = mybir.dt.float32r
BF16 = mybir.dt.bfloat16
ALU = mybir.AluOpType
ACT = mybir.ActivationFunctionType
AX_X = mybir.AxisListType.X

NB = 4
NT = 8
NG = 4
QA, KA, QB, KB = range(4)
WMA, WMB, WQA, WQB, WO = 0, 1024, 1536, 2048, 2304
WBLOB = 6400
SCALE = float(192) ** -0.5
LN_EPS = 1e-5
RMS_EPS = 1e-6


class Line:

    def __init__(self, ctx, nc, name):
        self.sem = ctx.enter_context(nc.semaphore(name))
        self.value = 0

    def next(self, step):
        self.value += step
        return (self.sem, self.value)


class Queues:

    def __init__(self):
        self.todo = {e: [] for e in ("tensor", "vector", "scalar", "gpsimd", "sync")}

    def put(self, engine, waits, issue, line=None, step=1):
        token = line.next(step) if line else None
        self.todo[engine].append((list(waits), issue, line.sem if line else None, step))
        return token

    def play(self, engine, eng):
        met = {}
        for waits, issue, sem, step in self.todo[engine]:
            for token in waits:
                if token is not None and met.get(id(token[0]), 0) < token[1]:
                    eng.wait_ge(*token)
                    met[id(token[0])] = token[1]
            if issue is None:
                continue
            last = issue(eng)
            if sem is not None:
                last.then_inc(sem, step)

    def run(self, nc):
        with nc.Block() as block:
            @block.sync
            def _(eng):
                self.play("sync", eng)

            @block.gpsimd
            def _(eng):
                self.play("gpsimd", eng)

            @block.scalar
            def _(eng):
                self.play("scalar", eng)

            @block.vector
            def _(eng):
                self.play("vector", eng)

            @block.tensor
            def _(eng):
                self.play("tensor", eng)


def prepare(nc, A, hscr, oscr, wscr):
    with ExitStack() as ctx:
        def sb(name, shape, dt=F32):
            return ctx.enter_context(nc.sbuf_tensor(name, shape, dt))

        def pb(name):
            return ctx.enter_context(nc.psum_tensor(name, [128, 512], F32))

        def line(name):
            return Line(ctx, nc, "p_" + name)

        q = Queues()
        put = q.put

        ident = sb("ident", [128, 128])
        rope = sb("rope0", [128, NT, 2, 64])
        nw = sb("nw", [128, 384])
        eps = sb("eps", [128, 2])
        wd = sb("wd", [128, 4, 384])
        wdh = sb("wdh", [128, 4, 384], F32R)
        wdl = sb("wdl", [128, 4, 384], F32R)
        fw = sb("fw", [128, 4, 512])
        fr = sb("fr", [128, 4, 512])
        fa = sb("fa", [128, 4, 512])
        wfh = sb("wfh", [128, 4, 512], F32R)
        wfl = sb("wfl", [128, 4, 512], F32R)
        X = sb("X", [128, 8, 512])
        XN = sb("XN", [128, 2, 512])
        XH = sb("XH", [128, 2, 512], F32R)
        XL = sb("XL", [128, 2, 512], F32R)
        XG = sb("XG", [128, 2, 512], BF16)
        XQ = sb("XQ", [128, 2, 512], F32R)
        ST = sb("ST", [128, 4, 6])
        MV = sb("MV", [128, 2, 4, 2])
        SM = sb("SM", [128, 2, 5, 4])
        CR = sb("CR", [128, 8, 384])
        SS = sb("SS", [128, 2, 12])
        RM = sb("RM", [128, 2, 5, 12])
        junk = sb("junk", [128, 192])
        C = sb("C", [128, 4, 512])
        KR = sb("KR", [128, 4, 4, 64])
        HT = sb("HT", [128, 4, 1280], F32R)
        OP = sb("OP", [128, 4, 512])

        pX = [pb("pX0"), pb("pX1")]
        pD = [pb("pD0"), pb("pD1")]
        pF = [pb("pF0"), pb("pF1")]
        pC = [pb("pC0"), pb("pC1")]

        ld_c = line("ld_c")
        ld_f = line("ld_f")
        ld_d = line("ld_d")
        ld_x = [line(f"ld_x{i}") for i in range(8)]
        st_h = [line(f"st_h{i}") for i in range(4)]
        st_o = [line(f"st_o{i}") for i in range(4)]
        l_wd = line("wd")
        l_fw = line("fw")
        l_act = line("act")
        l_dve = line("dve")
        l_pool = line("pool")
        l_pe = line("pe")
        l_eps = line("eps")

        x_tok = {}

        def load_x(t, after):
            x_tok[t] = put("sync", after, lambda e: e.dma_start(
                X[:, t % 8, :], A["x"][t // NT, (t % NT) * 128:(t % NT + 1) * 128, :]), ld_x[t % 8], 16)

        load_x(0, [])
        load_x(1, [])
        c_ld = None
        for dst, src in (
            (ident[:, :], A["ident"]),
            (rope[:, :, :, :], A["rope"].rearrange("(n p) a d -> p n a d", p=128)),
            (nw[:, 0:192], A["q_norm"].rearrange("(a n) -> a n", a=1).to_broadcast([128, 192])),
            (nw[:, 192:320], A["kv_norm"].rearrange("(a n) -> a n", a=1).to_broadcast([128, 128])),
            (nw[:, 320:384], A["k_pe_norm"].rearrange("(a n) -> a n", a=1).to_broadcast([128, 64])),
        ):
            c_ld = put("scalar", [], lambda e, d=dst, s=src: e.dma_start(d, s), ld_c, 16)
        for lo, w in ((0, "Wq_down"), (192, "Wkv_down"), (320, "Wk_pe")):
            n = {0: 192, 192: 128, 320: 64}[lo]
            d_ld = put("sync", [], lambda e, lo=lo, n=n, w=w: e.dma_start(
                wd[:, :, lo:lo + n], A[w].rearrange("(c p) n -> p c n", p=128)), ld_d, 16)
        load_x(2, [])
        load_x(3, [])
        for t in range(4, 8):
            load_x(t, [])
        for dst, w in ((fw, "weight"), (fr, "rram")):
            f_ld = put("sync", [], lambda e, d=dst, w=w: e.dma_start(
                d[:, :, :], A[w].rearrange("(c p) n -> p c n", p=128)), ld_f, 16)

        put("gpsimd", [], lambda e: e.memset(eps[:, 0:1], LN_EPS), l_eps)
        eps_t = put("gpsimd", [], lambda e: e.memset(eps[:, 1:2], RMS_EPS), l_eps)
        nwq = put("vector", [c_ld], lambda e: e.tensor_scalar(nw[:, 0:192], nw[:, 0:192], SCALE, None, ALU.mult),
                  l_wd)

        wd_hi = put("scalar", [d_ld], lambda e: e.activation(wdh[:, :, :], wd[:, :, :], ACT.Copy), l_wd2 := line("wd2"))
        wd_lo = put("vector", [wd_hi], lambda e: e.tensor_tensor(wdl[:, :, :], wd[:, :, :], wdh[:, :, :],
                                                                 ALU.subtract), l_wd)

        def fweights():
            a = put("gpsimd", [f_ld], lambda e: e.tensor_scalar(fa[:, :, :], fw[:, :, :], -0.2, -0.6, ALU.is_lt,
                                                                ALU.mult), l_fw0)
            b = put("vector", [a], lambda e: e.tensor_scalar(fw[:, :, :], fw[:, :, :], 0.2, 0.6, ALU.is_gt,
                                                             ALU.mult), l_fw)
            b = put("vector", [b], lambda e: e.tensor_tensor(fa[:, :, :], fa[:, :, :], fw[:, :, :], ALU.add), l_fw)
            b = put("vector", [b], lambda e: e.tensor_tensor(fa[:, :, :], fa[:, :, :], fr[:, :, :], ALU.add), l_fw)
            done = None
            free = [None, None]
            for c in range(4):
                bank = pF[c % 2]

                def tr(e, c=c, bank=bank):
                    for o in range(4):
                        m = e.transpose(bank[:, o * 128:(o + 1) * 128], fa[:, o, c * 128:(c + 1) * 128], ident[:, :])
                    return m
                t = put("tensor", [b, c_ld, free[c % 2]], tr, l_fw1)
                h = put("scalar", [t], lambda e, c=c, bank=bank: e.activation(
                    wfh[:, c, :], bank[:, :], ACT.Copy, scale=-0.5), l_fw2)
                done = free[c % 2] = put("vector", [h], lambda e, c=c, bank=bank: e.scalar_tensor_tensor(
                    out=wfl[:, c, :], in0=bank[:, :], scalar=-0.5, in1=wfh[:, c, :], op0=ALU.mult,
                    op1=ALU.subtract), l_fw)
            return done, free

        l_fw0, l_fw1, l_fw2 = line("fw0"), line("fw1"), line("fw2")

        T = NB * NT
        stat = {}
        s_free = {}
        xn = {}
        xh = {}
        xl = {}
        xq = {}
        xt = {}
        dmm = {}
        fmm = {}
        cr = {}
        out_dve = {}
        cnorm = {}
        kp = {}
        krd = {}
        ct = {}
        hh = {}
        hl = {}
        vv = {}
        rms = {}
        ostore = {}
        hstore = {}
        pf_free = [None, None]
        l_st, l_xn, l_xt, l_xh, l_xl, l_xq = (line(n) for n in ("st", "xn", "xt", "xh", "xl", "xq"))
        l_d, l_f, l_cr, l_o, l_ss, l_cn, l_kp, l_ct, l_hh, l_hl, l_vv = (
            line(n) for n in ("d", "f", "cr", "o", "ss", "cn", "kp", "ct", "hh", "hl", "vv"))
        l_sq = line("sq")

        def stats(quad):
            for k in range(4):
                t = 4 * quad + k
                a = put("vector", [x_tok[t], s_free.get(t - 4)], lambda e, t=t, k=k: e.bn_stats(
                    ST[:, k, :], X[:, t % 8, :]), l_st)
                a = put("vector", [a], lambda e, k=k: e.bn_aggr(MV[:, quad % 2, k, :], ST[:, k, :]), l_st)
                s_free[t] = a
            s = SM[:, quad % 2, :, :]
            var = MV[:, quad % 2, :, 1]
            r = put("scalar", [a, eps_t, rstd.get(quad - 2)], lambda e: e.activation(
                s[:, 0, :], var, ACT.Sqrt, bias=eps[:, 0:1]), l_sq)
            v = put("vector", [a], lambda e: e.tensor_scalar(s[:, 1, :], var, LN_EPS, None, ALU.add), l_st)
            y = put("vector", [r], lambda e: e.reciprocal(s[:, 2, :], s[:, 0, :]), l_st)
            a = put("vector", [y, v], lambda e: e.tensor_tensor(s[:, 3, :], s[:, 2, :], s[:, 2, :], ALU.mult), l_st)
            a = put("vector", [a], lambda e: e.tensor_tensor(s[:, 3, :], s[:, 3, :], s[:, 1, :], ALU.mult), l_st)
            a = put("vector", [a], lambda e: e.tensor_scalar(s[:, 3, :], s[:, 3, :], -0.5, 1.5, ALU.mult, ALU.add),
                    l_st)
            rstd[quad] = put("vector", [a], lambda e: e.tensor_tensor(s[:, 4, :], s[:, 2, :], s[:, 3, :],
                                                                      ALU.mult), l_st)

        rstd = {}

        def norm(t):
            m, k = (t // 4) % 2, t % 4
            xn[t] = put("vector", [rstd[t // 4], xt.get(t - 2)], lambda e: e.tensor_scalar(
                XN[:, t % 2, :], X[:, t % 8, :], MV[:, m, k, 0:1], SM[:, m, 4, k:k + 1], ALU.subtract, ALU.mult),
                l_xn)

        def turn(t):
            bank = pX[t % 2]

            def tr(e):
                for c in range(4):
                    m = e.transpose(bank[:, c * 128:(c + 1) * 128], XN[:, t % 2, c * 128:(c + 1) * 128], ident[:, :])
                return m
            xt[t] = put("tensor", [xn[t], c_ld, xq.get(t - 2)], tr, l_xt)
            xh[t] = put("scalar", [xt[t], dmm.get(t - 2)], lambda e: e.activation(
                XH[:, t % 2, :], bank[:, :], ACT.Copy), l_xh)
            xl[t] = put("vector", [xh[t]], lambda e: e.tensor_tensor(
                XL[:, t % 2, :], bank[:, :], XH[:, t % 2, :], ALU.subtract), l_xl)
            g = put("vector", [xt[t], fmm.get(t - 2)], lambda e: e.tensor_scalar(
                XG[:, t % 2, :], bank[:, :], 0.33, None, ALU.is_gt), l_xq)
            xq[t] = put("vector", [g], lambda e: e.scalar_tensor_tensor(
                out=XQ[:, t % 2, :], in0=bank[:, :], scalar=-0.33, in1=XG[:, t % 2, :], op0=ALU.is_lt,
                op1=ALU.subtract), l_xq)

        def project(t):
            bd, bf = pD[t % 2], pF[t % 2]

            def down(e):
                for c in range(4):
                    xhc, xlc = XH[:, t % 2, c * 128:(c + 1) * 128], XL[:, t % 2, c * 128:(c + 1) * 128]
                    e.matmul(bd[:, 0:384], xhc, wdh[:, c, :], start=(c == 0), stop=False)
                    e.matmul(bd[:, 0:384], xhc, wdl[:, c, :], start=False, stop=False)
                    m = e.matmul(bd[:, 0:384], xlc, wdh[:, c, :], start=False, stop=(c == 3))
                return m

            def ffn(e):
                for c in range(4):
                    xc = XQ[:, t % 2, c * 128:(c + 1) * 128]
                    e.matmul(bf[:, :], xc, wfh[:, c, :], start=(c == 0), stop=False)
                    m = e.matmul(bf[:, :], xc, wfl[:, c, :], start=False, stop=(c == 3))
                return m
            dmm[t] = put("tensor", [xl[t], wd_lo, cr.get(t - 2)], down, l_d)
            fmm[t] = put("tensor", [xq[t], f_done, out_dve.get(t - 2), pf_free[t % 2]], ffn, l_f)
            cr[t] = put("scalar", [dmm[t], cnorm.get(t - 8)], lambda e: e.activation(
                CR[:, t % 8, :], bd[:, 0:384], ACT.Copy), l_cr)
            out_dve[t] = put("vector", [fmm[t], ostore.get(t - 4)], lambda e: e.tensor_tensor(
                OP[:, t % 4, :], bf[:, :], X[:, t % 8, :], ALU.add), l_o)
            ostore[t] = put("sync", [out_dve[t]], lambda e: e.dma_start(oscr[t, :, :], OP[:, t % 4, :]),
                            st_o[t % 4], 16)
            if t + 8 < T:
                load_x(t + 8, [out_dve[t]])

        def squares(t):
            k, m = t % 4, (t // 4) % 2
            for j, (lo, hi) in enumerate(((0, 192), (192, 320), (320, 384))):
                a = put("scalar", [cr[t], rms.get(t // 4 - 2)] + ([sq_prev[0]] if sq_prev[0] else []),
                        lambda e, j=j, lo=lo, hi=hi: e.activation(
                    junk[:, 0:hi - lo], CR[:, t % 8, lo:hi], ACT.Square, scale=float(hi - lo) ** -0.5,
                    accum_out=SS[:, m, 3 * k + j:3 * k + j + 1]), l_ss)
                sq_prev[0] = a
            sqd[t] = a

        sq_prev = [None]
        sqd = {}

        def rms_quad(quad):
            m = quad % 2
            s = RM[:, m, :, :]
            ss = SS[:, m, :]
            r = put("scalar", [sqd[4 * quad + 3], rms.get(quad - 2)], lambda e: e.activation(
                s[:, 0, :], ss, ACT.Sqrt, bias=eps[:, 1:2]), l_sq)
            v = put("vector", [sqd[4 * quad + 3]], lambda e: e.tensor_scalar(s[:, 1, :], ss, RMS_EPS, None,
                                                                            ALU.add), l_st)
            y = put("vector", [r], lambda e: e.reciprocal(s[:, 2, :], s[:, 0, :]), l_st)
            a = put("vector", [y, v], lambda e: e.tensor_tensor(s[:, 3, :], s[:, 2, :], s[:, 2, :], ALU.mult), l_st)
            a = put("vector", [a], lambda e: e.tensor_tensor(s[:, 3, :], s[:, 3, :], s[:, 1, :], ALU.mult), l_st)
            a = put("vector", [a], lambda e: e.tensor_scalar(s[:, 3, :], s[:, 3, :], -0.5, 1.5, ALU.mult, ALU.add),
                    l_st)
            rms[quad] = put("vector", [a], lambda e: e.tensor_tensor(s[:, 4, :], s[:, 2, :], s[:, 3, :],
                                                                    ALU.mult), l_st)

        def compress(t):
            m, k, i, sl = (t // 4) % 2, t % 4, t % NT, t % 4
            r = [RM[:, m, 4, 3 * k + j:3 * k + j + 1] for j in range(3)]
            free = [rms[t // 4], nwq, ct.get(t - 4), vv.get(t - 4)]
            a = put("vector", free, lambda e: e.scalar_tensor_tensor(
                out=C[:, sl, 0:128], in0=CR[:, t % 8, 0:128], scalar=r[0], in1=nw[:, 0:128], op0=ALU.mult,
                op1=ALU.mult), l_cn)
            for o in (256, 320):
                a = put("vector", free, lambda e, o=o: e.scalar_tensor_tensor(
                    out=C[:, sl, o:o + 64], in0=CR[:, t % 8, 128:192], scalar=r[0], in1=nw[:, 128:192],
                    op0=ALU.mult, op1=ALU.mult), l_cn)
            a = put("vector", free, lambda e: e.scalar_tensor_tensor(
                out=C[:, sl, 128:256], in0=CR[:, t % 8, 192:320], scalar=r[1], in1=nw[:, 192:320], op0=ALU.mult,
                op1=ALU.mult), l_cn)
            cnorm[t] = put("vector", free + [kp.get(t - 4)], lambda e: e.scalar_tensor_tensor(
                out=KR[:, sl, 0, :], in0=CR[:, t % 8, 320:384], scalar=r[2], in1=nw[:, 320:384], op0=ALU.mult,
                op1=ALU.mult), l_cn)
            k0 = KR[:, sl, 0, :]
            p = put("gpsimd", [cnorm[t], c_ld], lambda e: e.tensor_tensor(KR[:, sl, 1, :], k0, rope[:, i, 0, :],
                                                                  ALU.mult), l_kp)
            p = put("gpsimd", [cnorm[t]], lambda e: e.tensor_tensor(
                KR[:, sl, 2, 0:32], KR[:, sl, 0, 32:64], rope[:, i, 1, 0:32], ALU.mult), l_kp)
            p = put("gpsimd", [cnorm[t]], lambda e: e.tensor_tensor(
                KR[:, sl, 2, 32:64], KR[:, sl, 0, 0:32], rope[:, i, 1, 32:64], ALU.mult), l_kp)
            for o in (384, 448):
                b = put("gpsimd", [p, ct.get(t - 4)], lambda e, o=o: e.tensor_tensor(
                    C[:, sl, o:o + 64], KR[:, sl, 1, :], KR[:, sl, 2, :], ALU.add), l_kp)
            kp[t] = b
            vh = put("gpsimd", [cnorm[t], hstore.get(t - 4)], lambda e: e.tensor_copy(
                HT[:, sl, 1024:1152], C[:, sl, 128:256]), l_vv)
            vv[t] = put("gpsimd", [vh], lambda e: e.tensor_tensor(
                HT[:, sl, 1152:1280], C[:, sl, 128:256], HT[:, sl, 1024:1152], ALU.subtract), l_vv)

        def turn_c(t):
            bank, sl = pC[t % 2], t % 4

            def tr(e):
                for c in range(4):
                    m = e.transpose(bank[:, c * 128:(c + 1) * 128], C[:, sl, c * 128:(c + 1) * 128], ident[:, :])
                return m
            ct[t] = put("tensor", [cnorm[t], kp[t], hl.get(t - 2)], tr, l_ct)
            hh[t] = put("scalar", [ct[t], hstore.get(t - 4)], lambda e: e.activation(
                HT[:, sl, 0:512], bank[:, :], ACT.Copy), l_hh)
            hl[t] = put("vector", [hh[t]], lambda e: e.tensor_tensor(
                HT[:, sl, 512:1024], bank[:, :], HT[:, sl, 0:512], ALU.subtract), l_hl)
            hstore[t] = put("sync", [hl[t], vv[t]], lambda e: e.dma_start(hscr[t, :, :], HT[:, sl, :].bitcast(F32)),
                            st_h[t % 4], 16)

        stats(0)
        norm(0)
        turn(0)
        f_done, pf_free = fweights()
        for t in range(T + 5):
            if t + 1 < T:
                if (t + 1) % 4 == 0:
                    stats((t + 1) // 4)
                norm(t + 1)
                turn(t + 1)
            if t < T:
                project(t)
                squares(t)
            if 4 <= t and t - 4 < T:
                if (t - 4) % 4 == 0:
                    rms_quad((t - 4) // 4)
                compress(t - 4)
            if t >= 5:
                turn_c(t - 5)
        for i in range(4):
            put("sync", [hstore[T - 4 + i], ostore[T - 4 + i]], None)
        q.run(nc)

    with ExitStack() as ctx:
        def sb(name, shape, dt=F32):
            return ctx.enter_context(nc.sbuf_tensor(name, shape, dt))

        def pb(name):
            return ctx.enter_context(nc.psum_tensor(name, [128, 512], F32))

        def line(name):
            return Line(ctx, nc, "w_" + name)

        q = Queues()
        put = q.put
        ident = sb("ident1", [128, 128])
        ua = sb("ua", [128, 2048])
        ub = sb("ub", [128, 2048])
        kv = sb("kv", [128, 2048])
        pa = sb("pa", [128, 1024])
        pbw = sb("pbw", [128, 1024])
        wo = sb("wo", [128, 2, 4, 512])
        tq = sb("tq", [128, 2, 1024])
        tk = sb("tk", [128, 2, 512])
        tmp = sb("tmp", [128, 2, 768], F32R)
        blob = sb("blob", [128, 2, WBLOB], F32R)
        bq = [pb("bq0"), pb("bq1")]
        bk = pb("bk")
        bm = [pb("bm0"), pb("bm1")]
        bw = [pb(f"bw{i}") for i in range(3)]
        ld = line("ld")
        ldo = [line("ldo0"), line("ldo1")]
        st = [line("st0"), line("st1")]
        l_t, l_e, l_m, l_mh, l_ml, l_w, l_wh, l_wl, l_p, l_ph = (line(n) for n in (
            "t", "e", "m", "mh", "ml", "w", "wh", "wl", "p", "ph"))
        wo_v = A["Wo"].rearrange("(h v) n -> v h n", v=128)
        wo_ld = {}

        def load_wo(g, after):
            wo_ld[g] = put("sync", after, lambda e: e.dma_start(wo[:, g % 2, :, :], wo_v[:, 4 * g:4 * g + 4, :]),
                           ldo[g % 2], 16)
        for dst, src in ((ident[:, :], A["ident"]), (kv[:, :], A["Wkv_up"]), (ua[:, :], A["Wq_up"][0:128, :]),
                         (ub[0:64, :], A["Wq_up"][128:192, :]), (ub[64:128, :], A["Wq_up"][128:192, :]),
                         (pa[:, :], A["Wq_pe"][0:128, :]), (pbw[0:64, :], A["Wq_pe"][128:192, :]),
                         (pbw[64:128, :], A["Wq_pe"][128:192, :])):
            ldd = put("sync", [], lambda e, d=dst, s=src: e.dma_start(d, s), ld, 16)
        load_wo(0, [])
        load_wo(1, [])
        bq_free, bk_free, bm_free, bw_free = [None, None], None, [None, None], [None] * 3
        t_done, m_last, w_last, stored = {}, {}, {}, {}
        nw_ = 0
        for g in range(NG):
            s = g % 2

            def tr_q(e, g=g):
                for h in range(4):
                    c = (4 * g + h) * 128
                    e.transpose(bq[0][:, h * 128:(h + 1) * 128], ua[:, c:c + 128], ident[:, :])
                    m = e.transpose(bq[1][:, h * 128:(h + 1) * 128], ub[:, c:c + 128], ident[:, :])
                return m

            def tr_k(e, g=g):
                for h in range(2):
                    c = (2 * g + h) * 128
                    e.transpose(bk[:, h * 128:(h + 1) * 128], kv[:, c:c + 128], ident[:, :])
                    m = e.transpose(bk[:, 256 + h * 128:384 + h * 128], kv[:, 1024 + c:1152 + c], ident[:, :])
                return m
            a = put("tensor", [ldd, bq_free[0], bq_free[1]], tr_q, l_t)
            b = put("tensor", [ldd, bk_free], tr_k, l_t)
            e0 = put("scalar", [a, m_last.get(g - 2)], lambda e, s=s: e.activation(
                tq[:, s, 0:512], bq[0][:, :], ACT.Copy), l_e)
            e1 = put("vector", [a, m_last.get(g - 2)], lambda e, s=s: e.tensor_copy(
                tq[:, s, 512:1024], bq[1][:, :]), l_p)
            e2 = put("scalar", [b, m_last.get(g - 2), w_last.get(g - 2)], lambda e, s=s: e.activation(
                tk[:, s, :], bk[:, :], ACT.Copy), l_e)
            bq_free, bk_free = [e0, e1], e2

            def mm_m(e, s=s):
                for h in range(4):
                    k = tk[:, s, (h // 2) * 128:(h // 2 + 1) * 128]
                    e.matmul(bm[0][:, h * 128:(h + 1) * 128], tq[:, s, h * 128:(h + 1) * 128], k,
                             start=True, stop=True)
                    m = e.matmul(bm[1][:, h * 128:(h + 1) * 128], tq[:, s, 512 + h * 128:640 + h * 128], k,
                                 start=True, stop=True)
                return m
            m_last[g] = put("tensor", [e0, e1, e2, bm_free[0], bm_free[1]], mm_m, l_m)
            free = stored.get(g - 2)
            h1 = put("scalar", [m_last[g], free], lambda e, s=s: e.activation(
                blob[:, s, WMA:WMA + 512], bm[0][:, :], ACT.Copy), l_mh)
            h2 = put("scalar", [m_last[g], free], lambda e, s=s: e.activation(
                blob[0:64, s, WMB:WMB + 512], bm[1][0:64, :], ACT.Copy), l_mh)
            h3 = put("scalar", [m_last[g], l_ml_prev.get(g - 2) if g else None] if g else [m_last[g]],
                     lambda e, s=s: e.activation(tmp[64:128, s, 0:512], bm[1][64:128, :], ACT.Copy), l_mh)
            lo1 = put("vector", [h1], lambda e, s=s: e.tensor_tensor(
                blob[:, s, WMA + 512:WMA + 1024], bm[0][:, :], blob[:, s, WMA:WMA + 512], ALU.subtract), l_ml)
            lo2 = put("vector", [h3, free], lambda e, s=s: e.tensor_tensor(
                blob[64:128, s, WMB:WMB + 512], bm[1][64:128, :], tmp[64:128, s, 0:512], ALU.subtract), l_ml)
            if g == 0:
                l_ml_prev = {}
            l_ml_prev[g] = lo2
            bm_free = [lo1, lo2]
            put("scalar", [ldd, free], lambda e, g=g, s=s: e.activation(
                blob[:, s, WQA:WQA + 256], pa[:, 256 * g:256 * g + 256], ACT.Copy), l_ph)
            put("scalar", [ldd, free], lambda e, g=g, s=s: e.activation(
                blob[0:64, s, WQB:WQB + 256], pbw[0:64, 256 * g:256 * g + 256], ACT.Copy), l_ph)
            p3 = put("scalar", [ldd, l_ml_prev.get(g - 2)], lambda e, g=g, s=s: e.activation(
                tmp[64:128, s, 512:768], pbw[64:128, 256 * g:256 * g + 256], ACT.Copy), l_ph)
            put("vector", [p3], lambda e, g=g, s=s: e.tensor_tensor(
                blob[:, s, WQA + 256:WQA + 512], pa[:, 256 * g:256 * g + 256], blob[:, s, WQA:WQA + 256],
                ALU.subtract), l_p)
            l_ml_prev[g] = qlo = put("vector", [p3], lambda e, g=g, s=s: e.tensor_tensor(
                blob[64:128, s, WQB:WQB + 256], pbw[64:128, 256 * g:256 * g + 256], tmp[64:128, s, 512:768],
                ALU.subtract), l_p)
            for h in range(4):
                bank = bw[nw_ % 3]
                wv = tk[:, s, 256 + (h // 2) * 128:384 + (h // 2) * 128]
                w = put("tensor", [e2, wo_ld[g], bw_free[nw_ % 3]], lambda e, h=h, s=s, bank=bank, wv=wv: e.matmul(
                    bank[:, :], wv, wo[:, s, h, :], start=True, stop=True), l_w)
                wh = put("scalar", [w, free], lambda e, h=h, s=s, bank=bank: e.activation(
                    blob[:, s, WO + 512 * h:WO + 512 * h + 512], bank[:, :], ACT.Copy), l_wh)
                wl = put("vector", [wh, free], lambda e, h=h, s=s, bank=bank: e.tensor_tensor(
                    blob[:, s, WO + 2048 + 512 * h:WO + 2560 + 512 * h], bank[:, :],
                    blob[:, s, WO + 512 * h:WO + 512 * h + 512], ALU.subtract), l_wl)
                bw_free[nw_ % 3] = wl
                nw_ += 1
            w_last[g] = w
            if g + 2 < NG:
                load_wo(g + 2, [w])
            stored[g] = put("sync", [h1, h2, lo1, lo2, p3, qlo, wh, wl], lambda e, g=g, s=s: e.dma_start(
                wscr[g, :, :], blob[:, s, :].bitcast(F32)), st[s], 16)
        for g in range(2, NG):
            put("sync", [stored[g]], None)
        q.run(nc)


def attend(nc, A, hscr, oscr, wscr, out):
    with ExitStack() as ctx:
        def sb(name, shape, dt=F32):
            return ctx.enter_context(nc.sbuf_tensor(name, shape, dt))

        def line(name):
            return Line(ctx, nc, "a_" + name)

        q = Queues()
        put = q.put
        ident = sb("ident2", [128, 128])
        identr = sb("identr", [128, 128], F32R)
        identb = sb("identb", [128, 128], BF16)
        maskf = sb("maskf", [128, 128])
        maskb = sb("maskb", [128, 128], BF16)
        rope = sb("rope", [128, NT, 2, 64])
        WB = sb("WB", [128, 2, WBLOB], F32R)
        H = sb("H", [128, 4, NT * 128], F32R)
        L = sb("L", [128, 4, NT * 128], F32R)
        V = sb("V", [128, NT, 256], F32R)
        ACC = sb("ACC", [128, NT, 512])
        P = sb("P", [128, 8, 1024])
        PH = sb("PH", [128, 2, 512], F32R)
        PL = sb("PL", [128, 2, 512], F32R)
        YH = sb("YH", [128, 2, 512], F32R)
        YL = sb("YL", [128, 2, 512], F32R)
        QH = sb("QH", [128, 2, 4, 256], F32R)
        QL = sb("QL", [128, 2, 4, 256], F32R)
        QP = sb("QP", [128, 2, 4, 256], F32R)
        R1 = sb("R1", [128, 2, 4, 64])
        R2 = sb("R2", [128, 2, 4, 64])
        QS = sb("QS", [128, 2, 4, 2, 64], F32R)
        nm = sb("nm", [128, 8])
        sm = sb("sm", [128, 8])
        rc = sb("rc", [128, 8])

        pS = [ctx.enter_context(nc.psum_tensor(f"pS{i}", [128, 1024], F32)) for i in range(2)]
        pT = [ctx.enter_context(nc.psum_tensor(f"pT{i}", [128, 512], F32)) for i in range(2)]
        pY = ctx.enter_context(nc.psum_tensor("pY", [128, 512], F32))
        pM = ctx.enter_context(nc.psum_tensor("pM", [128, 512], F32))

        ld_c = line("ld_c")
        ld_w = [line("ld_w0"), line("ld_w1")]
        ld_q = [line(f"ld_q{i}") for i in range(NT)]
        ld_k = [line(f"ld_k{i}") for i in range(NT)]
        ld_v = [line(f"ld_v{i}") for i in range(NT)]
        ld_o = [line(f"ld_o{i}") for i in range(NT)]
        st = [line(f"st{i}") for i in range(NT)]
        l_s, l_mx, l_ex, l_rc, l_sc, l_t, l_ph, l_pl, l_pv, l_yh, l_yl, l_c, l_acc = (line(n) for n in (
            "s", "mx", "ex", "rc", "sc", "t", "ph", "pl", "pv", "yh", "yl", "c", "acc"))
        l_m, l_qh, l_ql, l_r, l_rp, l_qs, l_qq, l_qp, l_k = (line(n) for n in (
            "m", "qh", "ql", "r", "rp", "qs", "qq", "qp", "k"))

        for dst, src in ((ident[:, :], A["ident"]), (maskf[:, :], A["mask"]),
                         (rope[:, :, :, :], A["rope"].rearrange("(n p) a d -> p n a d", p=128))):
            c_ld = put("scalar", [], lambda e, d=dst, s=src: e.dma_start(d, s), ld_c, 16)
        put("gpsimd", [c_ld], lambda e: e.tensor_copy(identb[:, :], ident[:, :]), l_k)
        put("gpsimd", [c_ld], lambda e: e.tensor_copy(identr[:, :], ident[:, :]), l_k)
        consts = put("gpsimd", [c_ld], lambda e: e.tensor_copy(maskb[:, :], maskf[:, :]), l_k)

        N = NB * NG * NT

        def where(n):
            return n // (NG * NT), n // NT % NG, n % NT

        wb = {}
        lq, lk, lv, lo_ = {}, {}, {}, {}
        s_tok, ex_tok, sc_tok = {}, {}, {}
        t_last, pv_last, c_tok, acc_tok, y_lo, y_hi = {}, {}, {}, {}, {}, {}
        st_tok = {}
        qprime = {}
        qpart = {}
        a_last = {}
        qdone = {}
        state = {"m": None, "S": 0, "P": 0, "pt": 0}
        s_free = [None, None]
        p_free = {}
        pt_lo = {}
        pt_pv = {}

        def load_w(gi, after):
            wb[gi] = put("sync", after, lambda e: e.dma_start(WB[:, gi % 2, :].bitcast(F32), wscr[gi % NG, :, :]),
                         ld_w[gi % 2], 16)

        h_v = hscr.rearrange("t p (z a n) -> t p z a n", a=2, n=128)

        def load_q(t, after):
            i = t % NT

            def one(e, dst, z):
                return e.dma_start(dst[:, 0:4:2, i * 128:(i + 1) * 128].bitcast(F32), h_v[t, :, z:z + 2, 0, :])
            put("sync", after, lambda e: one(e, H, 0), ld_q[i], 16)
            lq[t] = put("sync", [], lambda e: one(e, L, 2), ld_q[i], 16)

        def load_k(t, after):
            i = t % NT

            def one(e, dst, z):
                return e.dma_start(dst[:, 1:4:2, i * 128:(i + 1) * 128].bitcast(F32), h_v[t, :, z:z + 2, 1, :])
            put("sync", after, lambda e: one(e, H, 0), ld_k[i], 16)
            lk[t] = put("sync", [], lambda e: one(e, L, 2), ld_k[i], 16)

        def load_v(t, after):
            lv[t] = put("sync", after, lambda e: e.dma_start(V[:, t % NT, :].bitcast(F32), hscr[t, :, 1024:1280]),
                        ld_v[t % NT], 16)

        def load_o(t, after):
            lo_[t] = put("sync", after, lambda e: e.dma_start(ACC[:, t % NT, :], oscr[t, :, :]),
                         ld_o[t % NT], 16)

        later = []

        def item(fn):
            fn()
            for x in later:
                x[0] -= 1
            ready = [x for x in later if x[0] <= 0]
            for x in ready:
                later.remove(x)
            for x in ready:
                x[1]()

        def defer(k, fn):
            later.append([k, fn])

        def score(n, h):
            b, g, i = where(n)
            w = 128 * (i + 1)
            wide = max(256, w) if i != 4 else 768
            cuts = [(0, min(512, wide))] + ([(512, wide)] if wide > 512 else [])
            S = pS[state["S"] % 2]
            slot = state["S"] % 2
            state["S"] += 1
            ps = state["P"] % 8
            state["P"] += 1
            buf = (n // 2) % 2
            tq = slice((i % 2) * 128, (i % 2) * 128 + 128)
            qh, ql, qp = QH[:, buf, h, tq], QL[:, buf, h, tq], QP[:, buf, h, tq]

            def mm(e):
                for lo, hi in cuts:
                    o = S[:, lo:hi]
                    diag = lo <= 128 * i < hi
                    e.matmul(o, qh, H[:, KA, lo:hi], start=True, stop=False)
                    e.matmul(o, qh, L[:, KA, lo:hi], start=False, stop=False)
                    e.matmul(o, ql, H[:, KA, lo:hi], start=False, stop=False)
                    e.matmul(o, qp, H[:, KB, lo:hi], start=False, stop=False)
                    m = e.matmul(o, qp, L[:, KB, lo:hi], start=False, stop=not diag)
                    if diag:
                        m = e.matmul(S[:, 128 * i:128 * i + 128], identb[:, :], maskb[:, :], start=False, stop=True)
                return m
            base = b * NT
            waits = [lk[base + t] for t in range(wide // 128)] + [consts, s_free[slot]]
            waits += list(qdone[n // 2][h // 2]) + [qpart[n // 2][i % 2]]
            tok = put("tensor", waits, mm, l_s)
            a_last[n] = tok
            mx = put("vector", [tok, ex_tok.get(ps_last.get(ps))], lambda e: e.tensor_reduce(
                nm[:, ps:ps + 1], S[:, 0:w], AX_X, ALU.max, negate=True), l_mx)
            ex = put("scalar", [mx, p_free.get(ps), sc_tok.get(ps_last.get(ps))], lambda e: e.activation(
                P[:, ps, 0:w], S[:, 0:w], ACT.Exp, bias=nm[:, ps:ps + 1], accum_out=sm[:, ps:ps + 1]), l_ex)
            s_free[slot] = ex
            ex_tok[(n, h)] = ex
            ps_last[ps] = (n, h)

            def scale():
                r = put("vector", [ex], lambda e: e.reciprocal(rc[:, ps:ps + 1], sm[:, ps:ps + 1]), l_rc)
                sc_tok[(n, h)] = put("vector", [r], lambda e: e.tensor_scalar(
                    P[:, ps, 0:w], P[:, ps, 0:w], rc[:, ps:ps + 1], None, ALU.mult), l_sc)
            defer(2, scale)
            slots[(n, h)] = ps

        ps_last = {}
        slots = {}

        def turn(n, j):
            k = state["pt"]
            state["pt"] += 1
            bank = pT[k % 2]
            pts[(n, j)] = k

            def tr(e):
                for h in range(4):
                    m = e.transpose(bank[:, h * 128:(h + 1) * 128], P[:, slots[(n, h)], j * 128:(j + 1) * 128],
                                    ident[:, :])
                return m
            t = put("tensor", [sc_tok[(n, h)] for h in range(4)] + [pt_lo.get(k - 2)], tr, l_t)
            for h in range(4):
                p_free[slots[(n, h)]] = t
            hi = put("scalar", [t, pt_pv.get(k - 2)], lambda e: e.activation(
                PH[:, k % 2, :], bank[:, :], ACT.Copy), l_ph)
            pt_lo[k] = put("vector", [hi], lambda e: e.tensor_tensor(
                PL[:, k % 2, :], bank[:, :], PH[:, k % 2, :], ALU.subtract), l_pl)

        pts = {}

        def weigh(n, j):
            b, g, i = where(n)
            k = pts[(n, j)]
            s = k % 2

            def mm(e):
                e.matmul(pY[:, :], V[:, j, 0:128], PH[:, s, :], start=(j == 0), stop=False)
                e.matmul(pY[:, :], V[:, j, 128:256], PH[:, s, :], start=False, stop=False)
                return e.matmul(pY[:, :], V[:, j, 0:128], PL[:, s, :], start=False, stop=(j == i))
            pt_pv[k] = put("tensor", [pt_lo[k], lv[b * NT + j], y_lo.get(n - 1)], mm, l_pv)
            if j == i:
                y_hi[n] = put("scalar", [pt_pv[k], c_tok.get(n - 2)], lambda e: e.activation(
                    YH[:, n % 2, :], pY[:, :], ACT.Copy), l_yh)
                y_lo[n] = put("vector", [y_hi[n]], lambda e: e.tensor_tensor(
                    YL[:, n % 2, :], pY[:, :], YH[:, n % 2, :], ALU.subtract), l_yl)
                pv_last[n] = pt_pv[k]

        def combine(n):
            b, g, i = where(n)
            W = WB[:, (n // NT) % 2, :]
            t = b * NT + i

            def mm(e):
                for h in range(4):
                    yh, yl = YH[:, n % 2, h * 128:(h + 1) * 128], YL[:, n % 2, h * 128:(h + 1) * 128]
                    wh = W[:, WO + 512 * h:WO + 512 * h + 512]
                    wl = W[:, WO + 2048 + 512 * h:WO + 2560 + 512 * h]
                    e.matmul(pM[:, :], yh, wh, start=(h == 0), stop=False)
                    e.matmul(pM[:, :], yh, wl, start=False, stop=False)
                    m = e.matmul(pM[:, :], yl, wh, start=False, stop=(h == 3))
                return m
            c_tok[n] = put("tensor", [y_lo[n], state["m"], wb[n // NT]], mm, l_c)
            acc_tok[n] = put("vector", [c_tok[n], lo_[t], acc_tok.get(n - NT)], lambda e: e.tensor_tensor(
                ACC[:, i, :], pM[:, :], ACC[:, i, :], ALU.add), l_acc)
            state["m"] = acc_tok[n]
            if g == NG - 1:
                st_tok[t] = put("sync", [acc_tok[n]], lambda e: e.dma_start(
                    out[b, i * 128:(i + 1) * 128, :], ACC[:, i, :]), st[i], 16)
                if b + 1 < NB:
                    load_o(t + NT, [st_tok[t]])
            if i == NT - 1 and n // NT + 2 < NB * NG:
                load_w(n // NT + 2, [c_tok[n]])

        def up(pr, half):
            b, g, i = where(2 * pr)
            W = WB[:, (pr // 4) % 2, :]
            c = slice(i * 128, i * 128 + 256)

            def mm(e):
                for k in range(2):
                    h = 2 * half + k
                    o = pM[:, k * 256:(k + 1) * 256]
                    mh = W[:, WMA + 128 * h:WMA + 128 * h + 128]
                    ml = W[:, WMA + 512 + 128 * h:WMA + 640 + 128 * h]
                    mb = W[:, WMB + 128 * h:WMB + 128 * h + 128]
                    e.matmul(o, mh, H[:, QA, c], start=True, stop=False)
                    e.matmul(o, mh, L[:, QA, c], start=False, stop=False)
                    e.matmul(o, ml, H[:, QA, c], start=False, stop=False)
                    e.matmul(o, mb, H[:, QB, c], start=False, stop=False)
                    m = e.matmul(o, mb, L[:, QB, c], start=False, stop=True)
                return m
            t = b * NT + i
            tok = put("tensor", [wb[pr // 4], lq[t], lq[t + 1], state["m"]], mm, l_m)
            src = pM[:, :].rearrange("p (h n) -> p h n", h=2)
            d = (pr % 2, slice(2 * half, 2 * half + 2))
            free = a_last.get(2 * pr - 3)
            hi = put("scalar", [tok, free], lambda e: e.activation(QH[:, d[0], d[1], :], src, ACT.Copy), l_qh)
            lo = put("vector", [hi, free], lambda e: e.tensor_tensor(
                QL[:, d[0], d[1], :], src, QH[:, d[0], d[1], :], ALU.subtract), l_ql)
            state["m"] = lo
            qdone.setdefault(pr, {})[half] = (hi, lo)
            q_used[pr] = tok

        q_used = {}
        qs_tok = {}
        tr_last = {}

        def up_pe(pr):
            b, g, i = where(2 * pr)
            W = WB[:, (pr // 4) % 2, :]

            def mm(e):
                for k in range(2):
                    c = slice((i + k) * 128, (i + k + 1) * 128)
                    o = pM[:, k * 256:(k + 1) * 256]
                    wh, wl, wb_ = W[:, WQA:WQA + 256], W[:, WQA + 256:WQA + 512], W[:, WQB:WQB + 256]
                    e.matmul(o, H[:, QA, c], wh, start=True, stop=False)
                    e.matmul(o, H[:, QA, c], wl, start=False, stop=False)
                    e.matmul(o, L[:, QA, c], wh, start=False, stop=False)
                    e.matmul(o, H[:, QB, c], wb_, start=False, stop=False)
                    m = e.matmul(o, L[:, QB, c], wb_, start=False, stop=True)
                return m
            t = b * NT + i
            tok = put("tensor", [wb[pr // 4], lq[t], lq[t + 1], state["m"]], mm, l_m)
            src = pM[:, :].rearrange("p (t h d) -> p t h d", t=2, h=4)

            def tab(a, lo, hi):
                return rope[:, i:i + 2, a, lo:hi].unsqueeze(2).to_broadcast([128, 2, 4, hi - lo])
            free = qs_tok.get(pr - 1)
            a = put("vector", [tok, c_ld, rp_tok.get(pr - 1)], lambda e: e.tensor_tensor(
                R1[:, :, :, :], src, tab(0, 0, 64), ALU.mult), l_r)
            put("vector", [tok, rp_tok.get(pr - 1)], lambda e: e.tensor_tensor(
                R2[:, :, :, 0:32], src[:, :, :, 32:64], tab(1, 0, 32), ALU.mult), l_r)
            b_ = put("vector", [tok], lambda e: e.tensor_tensor(
                R2[:, :, :, 32:64], src[:, :, :, 0:32], tab(1, 32, 64), ALU.mult), l_r)
            state["m"] = b_
            r = put("gpsimd", [b_, free], lambda e: e.tensor_tensor(
                R1[:, :, :, :], R1[:, :, :, :], R2[:, :, :, :], ALU.add), l_rp)
            hi = put("scalar", [r, tr_last.get(pr - 1)], lambda e: e.activation(
                QS[:, :, :, 0, :], R1[:, :, :, :], ACT.Copy), l_qs)
            rp_tok[pr] = qs_tok[pr] = put("gpsimd", [hi, tr_last.get(pr - 1)], lambda e: e.tensor_tensor(
                QS[:, :, :, 1, :], R1[:, :, :, :], QS[:, :, :, 0, :], ALU.subtract), l_rp)

        rp_tok = {}

        def turn_pe(pr, k):
            def tr(e):
                for h in range(4):
                    m = e.transpose(pM[:, h * 128:(h + 1) * 128].bitcast(F32R),
                                    QS[:, k, h, :, :].rearrange("p a d -> p (a d)"), identr[:, :])
                return m
            tok = put("tensor", [qs_tok[pr], consts, state["m"]], tr, l_qq)
            tr_last[pr] = tok
            ev = put("scalar", [tok, a_last.get(2 * pr - 3)], lambda e: e.activation(
                QP[:, pr % 2, :, k * 128:(k + 1) * 128], pM[:, :].rearrange("p (h n) -> p h n", h=4), ACT.Copy),
                l_qp)
            state["m"] = ev
            qpart.setdefault(pr, {})[k] = ev

        load_w(0, [])
        load_q(0, [])
        load_q(1, [])
        load_k(0, [])
        load_k(1, [])
        load_v(0, [])
        load_w(1, [])
        load_o(0, [])
        load_v(1, [])
        load_o(1, [])
        for t in range(2, NT):
            load_q(t, [])
            load_k(t, [])
            load_v(t, [])
            load_o(t, [])

        def cost_b(n):
            return 8 if n >= 0 else 0

        for n in range(-3, N + 1):
            b, g, i = where(n)
            head = []
            fill = []
            u = n + 1
            if 0 <= u < N:
                head.append((1, lambda u=u: score(u, 0)))
                for h in range(1, 4):
                    fill.append((1, lambda u=u, h=h: score(u, h)))
            if 0 <= n - 1 < N:
                head.append((1, lambda n=n: combine(n - 1)))
            extra = []
            if (n + 3) % 2 == 0 and 0 <= n + 3 < N:
                pr = (n + 3) // 2
                extra = [lambda: up_pe(pr), lambda: up(pr, 0), lambda: up(pr, 1)]
            if (n + 2) % 2 == 0 and 0 <= n + 2 < N:
                pr2 = (n + 2) // 2
                extra = [lambda: turn_pe(pr2, 0), lambda: turn_pe(pr2, 1)]
            mixed = []
            for k in range(max(len(fill), len(extra))):
                if k < len(extra):
                    mixed.append(extra[k])
                if k < len(fill):
                    mixed.append(fill[k][1])
            blocks = []
            if 0 <= n < N:
                blocks = [lambda n=n: turn(n, 0)]
                for j in range(i + 1):
                    if j + 1 <= i:
                        blocks.append(lambda n=n, j=j: turn(n, j + 1))
                    blocks.append(lambda n=n, j=j: weigh(n, j))
            for _, fn in head:
                item(fn)
            while later and not mixed:
                item(lambda: None)
            na, nb_ = len(mixed), len(blocks)
            ia = ib = 0
            while ia < na or ib < nb_:
                if ib >= nb_ or (ia < na and (ia + 0.5) / na * 0.85 < (ib + 0.5) / nb_):
                    item(mixed[ia])
                    ia += 1
                else:
                    if any(0 <= n < N and (n, h) not in sc_tok for h in range(4)):
                        for x in list(later):
                            later.remove(x)
                            x[1]()
                    item(blocks[ib])
                    ib += 1
            if n >= 0 and b + 1 < NB and g == NG - 1 and n < N:
                if i == NT - 3:
                    pass
            if 0 <= n < N - 1 and b + 1 < NB and g == NG - 1:
                nxt = (b + 1) * NT
                if i % 2 == 0 and i < NT - 2 and False:
                    pass
                if i == NT - 4:
                    for t in range(0, NT - 2):
                        load_q(nxt + t, [q_used[(n + 2) // 2 - 0] if t >= 6 else q_used[n // 2 + 1]])
                if i == NT - 2:
                    for t in range(NT - 2, NT):
                        load_q(nxt + t, [q_used[n // 2]])
                    for t in range(NT):
                        load_k(nxt + t, [a_last[n + 1]])
            if 0 <= n < N and b + 1 < NB and g == NG - 1 and i == NT - 1:
                for t in range(NT):
                    load_v((b + 1) * NT + t, [pv_last[n]])
        for i in range(NT):
            put("sync", [st_tok[(NB - 1) * NT + i]], None)
        q.run(nc)


def build(nc, A, out):
    hscr = nc.dram_tensor("hscr", [NB * NT, 128, 1280], F32).ap()
    oscr = nc.dram_tensor("oscr", [NB * NT, 128, 512], F32).ap()
    wscr = nc.dram_tensor("wscr", [NG, 128, WBLOB], F32).ap()
    prepare(nc, A, hscr, oscr, wscr)
    attend(nc, A, hscr, oscr, wscr, out)


_INS = {"x": "L0_attn_x", "Wq_down": "L0_attn_Wq_down", "q_norm": "L0_attn_q_norm_w", "Wq_up": "L0_attn_Wq_up",
        "Wq_pe": "L0_attn_Wq_pe", "Wkv_down": "L0_attn_Wkv_down", "kv_norm": "L0_attn_kv_norm_w",
        "Wkv_up": "L0_attn_Wkv_up", "Wk_pe": "L0_attn_Wk_pe", "k_pe_norm": "L0_attn_k_pe_norm_w",
        "Wo": "L0_attn_Wo", "weight": "L0_ffn_weight", "rram": "L0_ffn_rram_variation"}


def constants():
    inv = np.float32(1.0) / np.power(np.float32(10000.0), np.arange(0, 64, 2, dtype=np.float32) / np.float32(64))
    ang = np.outer(np.arange(1024, dtype=np.float32), inv.astype(np.float32)).astype(np.float32)
    cos, sin = np.cos(ang), np.sin(ang)
    rope = np.stack([np.concatenate([cos, cos], 1), np.concatenate([-sin, sin], 1)], 1).astype(np.float32)
    k = np.arange(128)
    mask = np.where(k[None, :] > k[:, None], np.float32(-3.0e38), np.float32(0)).astype(np.float32)
    return {"ident": np.eye(128, dtype=np.float32), "rope": np.ascontiguousarray(rope), "mask": mask}


def kernel(**inputs):
    import concourse.bacc as _bacc
    from concourse import mybir as _mybir
    from concourse.bass_utils import run_bass_kernel_spmd as _run

    nc = _bacc.Bacc("TRN2", target_bir_lowering=False, num_devices=1)
    arrays, aps = {}, {}
    named = {k: np.ascontiguousarray(inputs[v]) for k, v in _INS.items()}
    named.update(constants())
    for k, a in named.items():
        arrays[f"in_{k}"] = a
        aps[k] = nc.dram_tensor(f"in_{k}", a.shape, _mybir.dt.from_np(a.dtype), kind="ExternalInput").ap()
    out = nc.dram_tensor("out_0", (4, 1024, 512), F32, kind="ExternalOutput").ap()
    build(nc, aps, out)
    r = _run(nc, [arrays], core_ids=[0])
    return r.results[0]["out_0"]
```

```python
from contextlib import ExitStack

import numpy as np

import concourse.bass as bass
from concourse import mybir

F32 = mybir.dt.float32
F32R = mybir.dt.float32r
BF16 = mybir.dt.bfloat16
ALU = mybir.AluOpType
ACT = mybir.ActivationFunctionType
AX_X = mybir.AxisListType.X

NB = 4
NT = 8
NG = 4
QA, KA, QB, KB = range(4)
WMA, WMB, WQA, WQB, WO = 0, 1024, 1536, 2048, 2304
WBLOB = 6400
SCALE = float(192) ** -0.5
LN_EPS = 1e-5
RMS_EPS = 1e-6


class Line:

    def __init__(self, ctx, nc, name):
        self.sem = ctx.enter_context(nc.semaphore(name))
        self.value = 0


class Task:

    def __init__(self, engine, waits, issue, line, step, after, busy, lag, key):
        self.engine, self.issue, self.line, self.step = engine, issue, line, step
        self.waits = [w for w in waits if w is not None]
        self.after = [w for w in after if w is not None]
        self.busy, self.lag, self.key = busy, lag, key
        self.token = None


class Queues:

    ENGINES = ("tensor", "vector", "scalar", "gpsimd", "sync")
    HOP = {"tensor": 197, "vector": 130, "scalar": 150, "gpsimd": 165, "sync": 100}
    TO_TENSOR = 60

    def __init__(self):
        self.tasks = []
        self.key = 0

    def put(self, engine, waits, issue, line=None, step=1, after=(), busy=100, lag=0, key=None):
        t = Task(engine, waits, issue, line, step, after, busy, lag,
                 (self.key if key is None else key, len(self.tasks)))
        self.tasks.append(t)
        return t

    def order(self):
        left, users = {}, {}
        for t in self.tasks:
            needs = set(t.waits) | set(t.after)
            left[t] = len(needs)
            for w in needs:
                users.setdefault(w, []).append(t)
        open_ = {e: [t for t in self.tasks if t.engine == e and not left[t]] for e in self.ENGINES}
        free = {e: 0.0 for e in self.ENGINES}
        when = {t: 0.0 for t in self.tasks}
        out = {e: [] for e in self.ENGINES}
        for _ in self.tasks:
            at, e = min((max(free[e], min(when[t] for t in open_[e])), e) for e in self.ENGINES if open_[e])
            t = min((t for t in open_[e] if when[t] <= at), key=lambda t: t.key)
            open_[e].remove(t)
            free[e] = at + t.busy
            out[e].append(t)
            if t.line is not None:
                t.line.value += t.step
                t.token = (t.line.sem, t.line.value)
            for u in users.get(t, ()):
                same = t.engine == u.engine and t not in u.waits
                when[u] = max(when[u], free[e] + (0 if same else t.lag + self.HOP[e] + (self.TO_TENSOR if u.engine == "tensor" else 0)))
                left[u] -= 1
                if not left[u]:
                    open_[u.engine].append(u)
        return out, max(free.values())

    def play(self, tasks, eng):
        met = {}
        for t in tasks:
            for w in t.waits:
                sem, value = w.token
                if met.get(id(sem), 0) < value:
                    eng.wait_ge(sem, value)
                    met[id(sem)] = value
            if t.issue is None:
                continue
            last = t.issue(eng)
            if t.line is not None:
                last.then_inc(t.line.sem, t.step)

    def run(self, nc):
        out, _ = self.order()
        with nc.Block() as block:
            @block.sync
            def _(eng):
                self.play(out["sync"], eng)

            @block.gpsimd
            def _(eng):
                self.play(out["gpsimd"], eng)

            @block.scalar
            def _(eng):
                self.play(out["scalar"], eng)

            @block.vector
            def _(eng):
                self.play(out["vector"], eng)

            @block.tensor
            def _(eng):
                self.play(out["tensor"], eng)


def dve(n):
    return 69 + 1.04 * n


def dve2(n):
    return 130 + 0.52 * n


def act(n, extra=0):
    return 52 + 0.832 * n + extra


def mm(*cols):
    return sum(n / 2.4 for n in cols)


def prepare(nc, A, hscr, oscr, wscr):
    with ExitStack() as ctx:
        def sb(name, shape, dt=F32):
            return ctx.enter_context(nc.sbuf_tensor(name, shape, dt))

        def pb(name):
            return ctx.enter_context(nc.psum_tensor(name, [128, 512], F32))

        def line(name):
            return Line(ctx, nc, "p_" + name)

        q = Queues()
        put = q.put

        ident = sb("ident", [128, 128])
        rope = sb("rope0", [128, NT, 2, 64])
        nw = sb("nw", [128, 384])
        eps = sb("eps", [128, 2])
        wd = sb("wd", [128, 4, 384])
        wdh = sb("wdh", [128, 4, 384], F32R)
        wdl = sb("wdl", [128, 4, 384], F32R)
        fw = sb("fw", [128, 4, 512])
        fr = sb("fr", [128, 4, 512])
        FT = sb("FT", [128, 2, 512])
        wfh = sb("wfh", [128, 4, 512], F32R)
        wfl = sb("wfl", [128, 4, 512], F32R)
        X = sb("X", [128, 8, 512])
        XN = sb("XN", [128, 2, 512])
        XH = sb("XH", [128, 2, 512], F32R)
        XL = sb("XL", [128, 2, 512], F32R)
        XG = sb("XG", [128, 2, 512], BF16)
        XQ = sb("XQ", [128, 2, 512], F32R)
        ST = sb("ST", [128, 4, 6])
        MV = sb("MV", [128, 2, 4, 2])
        SM = sb("SM", [128, 2, 5, 4])
        CR = sb("CR", [128, 8, 384])
        SS = sb("SS", [128, 2, 12])
        RM = sb("RM", [128, 2, 5, 12])
        junk = sb("junk", [128, 192])
        C = sb("C", [128, 3, 512])
        KR = sb("KR", [128, 3, 3, 64])
        HT = sb("HT", [128, 3, 1280], F32R)
        OP = sb("OP", [128, 2, 512])
        ua = sb("ua", [128, 512])
        ub = sb("ub", [128, 512])
        kv = sb("kv", [128, 2, 256])
        pa = sb("pa", [128, 256])
        pbw = sb("pbw", [128, 256])
        wo = sb("wo", [128, 4, 512])
        tq = sb("tq", [128, 1024])
        tk = sb("tk", [128, 512])
        tmp = sb("tmp", [128, 768], F32R)
        blob = sb("blob", [128, WBLOB], F32R)

        pX = [pb("pX0"), pb("pX1")]
        pD = [pb("pD0"), pb("pD1")]
        pF = pb("pF")
        pC = pb("pC")
        pW = [pb("pW0"), pb("pW1")]

        l_sq = line("sq")
        ld_i = line("ld_i")
        ld_c = line("ld_c")
        ld_f = line("ld_f")
        ld_d = line("ld_d")
        ld_w = line("ld_w")
        ld_wo = line("ld_wo")
        st_w = line("st_w")
        ld_x = [line(f"ld_x{i}") for i in range(8)]
        st_h = [line(f"st_h{i}") for i in range(3)]
        st_o = [line(f"st_o{i}") for i in range(2)]
        l_eps, l_nw, l_wdh, l_wdl, l_fw0, l_fw1, l_fw2, l_fw = (line(n) for n in (
            "eps", "nw", "wdh", "wdl", "fw0", "fw1", "fw2", "fw"))
        l_st, l_xn, l_xt, l_xh, l_xl, l_xq = (line(n) for n in ("st", "xn", "xt", "xh", "xl", "xq"))
        l_d, l_f, l_cr, l_o, l_ss, l_cn, l_kp, l_ct, l_hh, l_hl, l_vv = (
            line(n) for n in ("d", "f", "cr", "o", "ss", "cn", "kp", "ct", "hh", "hl", "vv"))
        l_wt, l_we, l_wc, l_wm, l_wh, l_wl = (line(n) for n in ("wt", "we", "wc", "wm", "wh", "wl"))

        x_tok = {}

        def dma(waits, dst, src, ln, after=()):
            return put("sync", waits, lambda e: e.dma_start(dst, src), ln, 16, after=after,
                       busy=60 + dst.size() / 90, lag=2000)

        def load_x(t, waits):
            x_tok[t] = dma(waits, X[:, t % 8, :], A["x"][t // NT, (t % NT) * 128:(t % NT + 1) * 128, :],
                           ld_x[t % 8])

        q.key = -10
        id_ld = put("scalar", [], lambda e: e.dma_start(ident[:, :], A["ident"]), ld_i, 16, busy=60, lag=2500)
        for t in range(4):
            load_x(t, [])
        d_ld = None
        for lo, n, w in ((0, 192, "Wq_down"), (192, 128, "Wkv_down"), (320, 64, "Wk_pe")):
            d_ld = dma([], wd[:, :, lo:lo + n], A[w].rearrange("(c p) n -> p c n", p=128), ld_d, [d_ld])
        c_ld = None
        for dst, src in (
            (nw[:, 0:192], A["q_norm"].rearrange("(a n) -> a n", a=1).to_broadcast([128, 192])),
            (nw[:, 192:320], A["kv_norm"].rearrange("(a n) -> a n", a=1).to_broadcast([128, 128])),
            (nw[:, 320:384], A["k_pe_norm"].rearrange("(a n) -> a n", a=1).to_broadcast([128, 64])),
            (rope[:, :, :, :], A["rope"].rearrange("(n p) a d -> p n a d", p=128)),
        ):
            c_ld = put("scalar", [], lambda e, d=dst, s=src: e.dma_start(d, s), ld_c, 16, after=[c_ld], busy=60,
                       lag=9000)
        f_ld = None
        for dst, w in ((fw, "weight"), (fr, "rram")):
            f_ld = dma([], dst[:, :, :], A[w].rearrange("(c p) n -> p c n", p=128), ld_f, [f_ld])
        for t in range(4, 8):
            load_x(t, [])

        put("gpsimd", [], lambda e: e.memset(eps[:, 0:1], LN_EPS), l_eps)
        eps_t = put("gpsimd", [], lambda e: e.memset(eps[:, 1:2], RMS_EPS), l_eps)
        put("scalar", [eps_t], lambda e: e.activation(junk[:, 0:1], eps[:, 0:1], ACT.Sqrt), l_sq, busy=1500, key=-20)
        nwq = put("vector", [c_ld], lambda e: e.tensor_scalar(nw[:, 0:192], nw[:, 0:192], SCALE, None, ALU.mult),
                  l_nw)

        wd_hi = put("scalar", [d_ld], lambda e: e.activation(wdh[:, :, :], wd[:, :, :], ACT.Copy), l_wdh,
                    busy=act(1536))
        wd_lo = put("vector", [wd_hi], lambda e: e.tensor_tensor(wdl[:, :, :], wd[:, :, :], wdh[:, :, :],
                                                                 ALU.subtract), l_wdl, busy=dve(1536))

        q.key = 0.5
        ternary = []
        for c in range(4):
            g = ternary[c - 2] if c >= 2 else None
            a = put("vector", [f_ld, g], lambda e, c=c: e.tensor_scalar(
                FT[:, c % 2, :], fw[:, c, :], -0.2, -0.6, ALU.is_lt, ALU.mult), l_fw, busy=dve2(512))
            b = put("vector", [f_ld], lambda e, c=c: e.tensor_scalar(
                fw[:, c, :], fw[:, c, :], 0.2, 0.6, ALU.is_gt, ALU.mult), l_fw, busy=dve2(512), after=[a])
            b = put("vector", [a, b], lambda e, c=c: e.tensor_tensor(
                fw[:, c, :], fw[:, c, :], FT[:, c % 2, :], ALU.add), l_fw, busy=dve(512))
            ternary.append(put("vector", [b], lambda e, c=c: e.tensor_tensor(
                fr[:, c, :], fr[:, c, :], fw[:, c, :], ALU.add), l_fw, busy=dve(512)))
        w_free = [None, None]
        w_turn = 0
        for c in range(4):
            bank = pW[w_turn % 2]

            def tr(e, c=c, bank=bank):
                for o in range(4):
                    m = e.transpose(bank[:, o * 128:(o + 1) * 128], fr[:, o, c * 128:(c + 1) * 128], ident[:, :])
                return m
            t = put("tensor", ternary + [id_ld, w_free[w_turn % 2]], tr, l_fw1, busy=440)
            h = put("scalar", [t], lambda e, c=c, bank=bank: e.activation(
                wfh[:, c, :], bank[:, :], ACT.Copy, scale=-0.5), l_fw2, busy=act(512))
            f_done = w_free[w_turn % 2] = put("vector", [h], lambda e, c=c, bank=bank: e.scalar_tensor_tensor(
                out=wfl[:, c, :], in0=bank[:, :], scalar=-0.5, in1=wfh[:, c, :], op0=ALU.mult,
                op1=ALU.subtract), l_fw, busy=dve(560))
            w_turn += 1

        T = NB * NT
        rstd, xn, xq, xt, xh, xl, dmm, fmm, cr, od = ({} for _ in range(10))
        cn, kp, ct, hh, hl, vv, rms, ostore, hstore, sqd = ({} for _ in range(10))
        normed = {}
        bn, oe = {}, {}
        l_oe = line("oe")

        def newton(s, var, eps_c, add, busy, first, free, n):
            r = put("scalar", [first, eps_t, free], lambda e: e.activation(
                s[:, 0, :], var, ACT.Sqrt, bias=eps_c), l_sq, busy=200)
            v = put("vector", [first, free], lambda e: e.tensor_scalar(s[:, 1, :], var, add, None, ALU.add), l_st,
                    busy=busy)
            y = put("vector", [r], lambda e: e.reciprocal(s[:, 2, :], s[:, 0, :]), l_st, busy=busy)
            a = put("vector", [y], lambda e: e.tensor_tensor(s[:, 3, :], s[:, 2, :], s[:, 2, :], ALU.mult), l_st,
                    busy=busy)
            a = put("vector", [a, v], lambda e: e.tensor_tensor(s[:, 3, :], s[:, 3, :], s[:, 1, :], ALU.mult), l_st,
                    busy=busy)
            a = put("vector", [a], lambda e: e.tensor_scalar(s[:, 3, :], s[:, 3, :], -0.5, 1.5, ALU.mult, ALU.add),
                    l_st, busy=busy)
            return put("vector", [a], lambda e: e.tensor_tensor(s[:, 4, :], s[:, 2, :], s[:, 3, :], ALU.mult), l_st,
                       busy=busy)

        def stats(quad):
            m = quad % 2
            for k in range(4):
                t = 4 * quad + k
                a = put("vector", [x_tok[t], bn.get(t - 4)], lambda e, t=t, k=k: e.bn_stats(
                    ST[:, k, :], X[:, t % 8, :]), l_st, busy=600)
                bn[t] = put("vector", [a, xn.get(t - 8)], lambda e, k=k: e.bn_aggr(MV[:, m, k, :], ST[:, k, :]),
                            l_st, busy=80)
            rstd[quad] = newton(SM[:, m, :, :], MV[:, m, :, 1], eps[:, 0:1], LN_EPS, 75, bn[4 * quad + 3],
                                xn.get(4 * quad - 5), 4)

        def norm(t):
            m, k = (t // 4) % 2, t % 4
            xn[t] = put("vector", [rstd[t // 4], xt.get(t - 2)], lambda e: e.tensor_scalar(
                XN[:, t % 2, :], X[:, t % 8, :], MV[:, m, k, 0:1], SM[:, m, 4, k:k + 1], ALU.subtract, ALU.mult),
                l_xn, busy=dve2(512), after=[xn.get(t - 1)])

        def turn(t):
            bank = pX[t % 2]

            def tr(e):
                for c in range(4):
                    m = e.transpose(bank[:, c * 128:(c + 1) * 128], XN[:, t % 2, c * 128:(c + 1) * 128], ident[:, :])
                return m
            xt[t] = put("tensor", [xn[t], id_ld, xq.get(t - 2), xl.get(t - 2)], tr, l_xt, busy=440)
            xh[t] = put("scalar", [xt[t], dmm.get(t - 2)], lambda e: e.activation(
                XH[:, t % 2, :], bank[:, :], ACT.Copy), l_xh, busy=act(512))
            g = put("vector", [xh[t]], lambda e: e.tensor_scalar(
                XG[:, t % 2, :], bank[:, :], 0.33, None, ALU.is_gt), l_xq, busy=dve(512))
            xq[t] = put("vector", [g, xh[t], fmm.get(t - 2)], lambda e: e.scalar_tensor_tensor(
                out=XQ[:, t % 2, :], in0=bank[:, :], scalar=-0.33, in1=XG[:, t % 2, :], op0=ALU.is_lt,
                op1=ALU.subtract), l_xq, busy=dve(512))
            xl[t] = put("vector", [xh[t], dmm.get(t - 2)], lambda e: e.tensor_tensor(
                XL[:, t % 2, :], bank[:, :], XH[:, t % 2, :], ALU.subtract), l_xl, busy=dve(512))

        def project(t):
            bd = pD[t % 2]

            def down(e):
                for c in range(4):
                    xhc, xlc = XH[:, t % 2, c * 128:(c + 1) * 128], XL[:, t % 2, c * 128:(c + 1) * 128]
                    e.matmul(bd[:, 0:384], xhc, wdh[:, c, :], start=(c == 0), stop=False)
                    e.matmul(bd[:, 0:384], xhc, wdl[:, c, :], start=False, stop=False)
                    m = e.matmul(bd[:, 0:384], xlc, wdh[:, c, :], start=False, stop=(c == 3))
                return m

            def ffn(e):
                for c in range(4):
                    xc = XQ[:, t % 2, c * 128:(c + 1) * 128]
                    e.matmul(pF[:, :], xc, wfh[:, c, :], start=(c == 0), stop=False)
                    m = e.matmul(pF[:, :], xc, wfl[:, c, :], start=False, stop=(c == 3))
                return m
            dmm[t] = put("tensor", [xl[t], wd_lo, cr.get(t - 2)], down, l_d, busy=mm(*[384] * 12))
            fmm[t] = put("tensor", [xq[t], f_done, oe.get(t - 1)], ffn, l_f, busy=mm(*[512] * 8))
            cr[t] = put("scalar", [dmm[t], normed.get(t - 8)], lambda e: e.activation(
                CR[:, t % 8, :], bd[:, 0:384], ACT.Copy), l_cr, busy=act(384))
            oe[t] = put("scalar", [fmm[t], ostore.get(t - 2)], lambda e: e.activation(
                OP[:, t % 2, :], pF[:, :], ACT.Copy), l_oe, busy=act(512))
            od[t] = put("gpsimd", [oe[t]], lambda e: e.tensor_tensor(
                OP[:, t % 2, :], OP[:, t % 2, :], X[:, t % 8, :], ALU.add), l_o, busy=1225)
            ostore[t] = dma([od[t]], oscr[t, :, :], OP[:, t % 2, :], st_o[t % 2])
            if t + 8 < T:
                load_x(t + 8, [od[t], bn[t], xn[t]])

        def squares(t):
            k, m = t % 4, (t // 4) % 2
            for j, (lo, hi) in enumerate(((0, 192), (192, 320), (320, 384))):
                sqd[t] = put("scalar", [cr[t], rms.get(t // 4 - 2), sqd.get(t, sqd.get(t - 1))],
                             lambda e, j=j, lo=lo, hi=hi: e.activation(
                    junk[:, 0:hi - lo], CR[:, t % 8, lo:hi], ACT.Square, scale=float(hi - lo) ** -0.5,
                    accum_out=SS[:, m, 3 * k + j:3 * k + j + 1]), l_ss, busy=act(hi - lo, 180))

        def rms_quad(quad):
            m = quad % 2
            rms[quad] = newton(RM[:, m, :, :], SS[:, m, :], eps[:, 1:2], RMS_EPS, 80, sqd[4 * quad + 3],
                               normed.get(4 * quad - 5), 12)

        def compress(t):
            m, k, i, sl = (t // 4) % 2, t % 4, t % NT, t % 3
            r = [RM[:, m, 4, 3 * k + j:3 * k + j + 1] for j in range(3)]
            free = [rms[t // 4], nwq, ct.get(t - 3)]
            a = cn.get(t - 1)
            for dst, lo, hi, rr, more in (
                (C[:, sl, 0:128], 0, 128, r[0], []), (C[:, sl, 256:320], 128, 192, r[0], []),
                (C[:, sl, 128:256], 192, 320, r[1], [vv.get(t - 3)]),
                (KR[:, sl, 0, :], 320, 384, r[2], [kp.get(t - 3)]),
            ):
                a = put("vector", free + more, lambda e, dst=dst, lo=lo, hi=hi, rr=rr: e.scalar_tensor_tensor(
                    out=dst, in0=CR[:, t % 8, lo:hi], scalar=rr, in1=nw[:, lo:hi], op0=ALU.mult, op1=ALU.mult),
                    l_cn, busy=dve(hi - lo), after=[a])
            cn[t] = normed[t] = a
            kb = put("gpsimd", [a, ct.get(t - 3)], lambda e: e.tensor_copy(C[:, sl, 320:384], C[:, sl, 256:320]),
                     l_kp, busy=350)
            p = kb
            for dst, s0, s1 in (
                (KR[:, sl, 1, :], KR[:, sl, 0, :], rope[:, i, 0, :]),
                (KR[:, sl, 2, 0:32], KR[:, sl, 0, 32:64], rope[:, i, 1, 0:32]),
                (KR[:, sl, 2, 32:64], KR[:, sl, 0, 0:32], rope[:, i, 1, 32:64]),
            ):
                p = put("gpsimd", [a, c_ld, kp.get(t - 3)], lambda e, dst=dst, s0=s0, s1=s1: e.tensor_tensor(
                    dst, s0, s1, ALU.mult), l_kp, busy=250, after=[p])
            b = p
            for o in (384, 448):
                b = put("gpsimd", [p, ct.get(t - 3)], lambda e, o=o: e.tensor_tensor(
                    C[:, sl, o:o + 64], KR[:, sl, 1, :], KR[:, sl, 2, :], ALU.add), l_kp, busy=280, after=[b])
            kp[t] = b
            vh = put("gpsimd", [a, hstore.get(t - 3)], lambda e: e.tensor_copy(
                HT[:, sl, 1024:1152], C[:, sl, 128:256]), l_vv, busy=550)
            vv[t] = put("gpsimd", [vh], lambda e: e.tensor_tensor(
                HT[:, sl, 1152:1280], C[:, sl, 128:256], HT[:, sl, 1024:1152], ALU.subtract), l_vv, busy=430)

        def turn_c(t):
            sl = t % 3

            def tr(e):
                for c in range(4):
                    m = e.transpose(pC[:, c * 128:(c + 1) * 128], C[:, sl, c * 128:(c + 1) * 128], ident[:, :])
                return m
            ct[t] = put("tensor", [cn[t], kp[t], hl.get(t - 1), id_ld], tr, l_ct, busy=440)
            hh[t] = put("scalar", [ct[t], hstore.get(t - 3)], lambda e: e.activation(
                HT[:, sl, 0:512], pC[:, :], ACT.Copy), l_hh, busy=act(512))
            hl[t] = put("vector", [hh[t]], lambda e: e.tensor_tensor(
                HT[:, sl, 512:1024], pC[:, :], HT[:, sl, 0:512], ALU.subtract), l_hl, busy=dve(512))
            hstore[t] = dma([hl[t], vv[t]], hscr[t, :, :], HT[:, sl, :].bitcast(F32), st_h[sl])

        wo_v = A["Wo"].rearrange("(h v) n -> v h n", v=128)
        kv_v = A["Wkv_up"].rearrange("p (a n) -> p a n", a=2)
        wst = {"t": [], "m": None, "w": None, "q": [], "p": None, "store": None, "ld": None, "turn": w_turn}

        def weights(g):
            c4, c2 = slice(512 * g, 512 * g + 512), slice(256 * g, 256 * g + 256)
            ldd = wst["ld"]
            for dst, src, w in ((kv[:, :, :], kv_v[:, :, c2], "t"), (ua[:, :], A["Wq_up"][0:128, c4], "t"),
                                (ub[0:64, :], A["Wq_up"][128:192, c4], "t"),
                                (ub[64:128, :], A["Wq_up"][128:192, c4], "t"),
                                (pa[:, :], A["Wq_pe"][0:128, c2], "q"), (pbw[0:64, :], A["Wq_pe"][128:192, c2], "q"),
                                (pbw[64:128, :], A["Wq_pe"][128:192, c2], "q")):
                ldd = dma(wst[w], dst, src, ld_w, [ldd])
            wst["ld"] = ldd
            wo_ld = dma([wst["w"]], wo[:, :, :], wo_v[:, 4 * g:4 * g + 4, :], ld_wo)
            store = wst["store"]

            def bank():
                k = wst["turn"] % 2
                wst["turn"] += 1
                return pW[k], w_free[k], k

            def tr(srcs):
                pk, free, k = bank()

                def go(e):
                    for j, src in enumerate(srcs):
                        m = e.transpose(pk[:, j * 128:(j + 1) * 128], src, ident[:, :])
                    return m
                wst["p"] = put("tensor", [ldd, id_ld, free], go, l_wt, busy=440, after=[wst["p"]])
                return pk, wst["p"], k
            pk, t0, k = tr([ua[:, h * 128:(h + 1) * 128] for h in range(4)])
            e0 = w_free[k] = put("scalar", [t0, wst["m"]], lambda e, pk=pk: e.activation(
                tq[:, 0:512], pk[:, :], ACT.Copy), l_we, busy=act(512))
            pk, t1, k = tr([ub[:, h * 128:(h + 1) * 128] for h in range(4)])
            e1 = w_free[k] = put("scalar", [t1, wst["m"]], lambda e, pk=pk: e.activation(
                tq[:, 512:1024], pk[:, :], ACT.Copy), l_we, busy=act(512))
            pk, t2, k = tr([kv[:, a, h * 128:(h + 1) * 128] for a in range(2) for h in range(2)])
            e2 = w_free[k] = put("scalar", [t2, wst["m"], wst["w"]], lambda e, pk=pk: e.activation(
                tk[:, :], pk[:, :], ACT.Copy), l_we, busy=act(512))
            wst["t"] = [t2]

            def products(off):
                pk, free, k = bank()

                def go(e):
                    for h in range(4):
                        m = e.matmul(pk[:, h * 128:(h + 1) * 128], tq[:, off + h * 128:off + (h + 1) * 128],
                                     tk[:, (h // 2) * 128:(h // 2 + 1) * 128], start=True, stop=True)
                    return m
                wst["p"] = put("tensor", [e0, e1, e2, free], go, l_wm, busy=880, after=[wst["p"]])
                return pk, wst["p"], k

            def two_parts(pk, tok, k, hi, lo):
                a = put("scalar", [tok, store], lambda e: e.activation(hi, pk[:, :], ACT.Copy), l_wh,
                        busy=act(512))
                w_free[k] = put("vector", [a, store], lambda e: e.tensor_tensor(lo, pk[:, :], hi, ALU.subtract),
                                l_wl, busy=dve(512))
                return [a, w_free[k]]

            def stacked(src, n, at, off, tok, free):
                a = put("scalar", [tok, store], lambda e: e.activation(
                    blob[0:64, at:at + n], src[0:64, :], ACT.Copy), l_wh, busy=act(n))
                b = put("scalar", [tok, free], lambda e: e.activation(
                    tmp[64:128, off:off + n], src[64:128, :], ACT.Copy), l_wh, busy=act(n))
                c = put("vector", [a, b, store], lambda e: e.tensor_tensor(
                    blob[64:128, at:at + n], src[64:128, :], tmp[64:128, off:off + n], ALU.subtract), l_wl,
                    busy=dve(n))
                return [a, b, c]
            done = []
            pk, t3, k = products(0)
            done += two_parts(pk, t3, k, blob[:, WMA:WMA + 512], blob[:, WMA + 512:WMA + 1024])
            pk, t4, k = products(512)
            x = stacked(pk, 512, WMB, 0, t4, wst.get("tmp"))
            w_free[k] = x[-1]
            done += x
            wst["m"] = t4
            a = put("scalar", [ldd, store], lambda e: e.activation(blob[:, WQA:WQA + 256], pa[:, :], ACT.Copy), l_wh,
                    busy=act(256))
            b = put("vector", [a, store], lambda e: e.tensor_tensor(
                blob[:, WQA + 256:WQA + 512], pa[:, :], blob[:, WQA:WQA + 256], ALU.subtract), l_wl, busy=dve(256))
            x = stacked(pbw, 256, WQB, 512, ldd, wst.get("tmp"))
            done += [a, b] + x
            wst["tmp"] = x[-1]
            wst["q"] = [b, x[-1]]
            for h in range(4):
                pk, free, k = bank()
                w = put("tensor", [e2, wo_ld, free], lambda e, h=h, pk=pk: e.matmul(
                    pk[:, :], tk[:, 256 + (h // 2) * 128:384 + (h // 2) * 128], wo[:, h, :], start=True, stop=True),
                    l_wm, busy=860, after=[wst["p"]])
                wst["p"] = w
                done += two_parts(pk, w, k, blob[:, WO + 512 * h:WO + 512 * h + 512],
                                  blob[:, WO + 2048 + 512 * h:WO + 2560 + 512 * h])
            wst["w"] = w
            wst["store"] = dma(done, wscr[g, :, :], blob[:, :].bitcast(F32), st_w)

        for quad in range(T // 4 + 1):
            if quad < T // 4:
                q.key = 4 * quad
                stats(quad)
                for t in range(4 * quad, 4 * quad + 4):
                    q.key = t
                    norm(t)
                    turn(t)
                    project(t)
                    squares(t)
            if 1 <= quad:
                q.key = 4 * quad
                rms_quad(quad - 1)
                for t in range(4 * quad - 4, 4 * quad):
                    q.key = t + 4.5
                    compress(t)
                    turn_c(t)
            if 1 <= quad <= NG:
                q.key = 4 * quad + 6
                weights(quad - 1)
        q.key = 1000
        for t in (hstore[T - 3], hstore[T - 2], hstore[T - 1], ostore[T - 2], ostore[T - 1], wst["store"]):
            put("sync", [t], None)
        q.run(nc)


def attend(nc, A, hscr, oscr, wscr, out):
    with ExitStack() as ctx:
        def sb(name, shape, dt=F32):
            return ctx.enter_context(nc.sbuf_tensor(name, shape, dt))

        def line(name):
            return Line(ctx, nc, "a_" + name)

        q = Queues()
        put = q.put
        ident = sb("ident2", [128, 128])
        identr = sb("identr", [128, 128], F32R)
        identb = sb("identb", [128, 128], BF16)
        maskf = sb("maskf", [128, 128])
        maskb = sb("maskb", [128, 128], BF16)
        rope = sb("rope", [128, NT, 2, 64])
        WB = sb("WB", [128, 2, WBLOB], F32R)
        H = sb("H", [128, 4, NT * 128], F32R)
        L = sb("L", [128, 4, NT * 128], F32R)
        V = sb("V", [128, NT, 256], F32R)
        ACC = sb("ACC", [128, NT, 512])
        P = sb("P", [128, 8, 1024])
        PH = sb("PH", [128, 2, 512], F32R)
        PL = sb("PL", [128, 2, 512], F32R)
        YH = sb("YH", [128, 2, 512], F32R)
        YL = sb("YL", [128, 2, 512], F32R)
        QH = sb("QH", [128, 2, 4, 256], F32R)
        QL = sb("QL", [128, 2, 4, 256], F32R)
        QP = sb("QP", [128, 2, 4, 256], F32R)
        R1 = sb("R1", [128, 2, 4, 64])
        R2 = sb("R2", [128, 2, 4, 64])
        QS = sb("QS", [128, 2, 4, 2, 64], F32R)
        nm = sb("nm", [128, 8])
        sm = sb("sm", [128, 8])
        rc = sb("rc", [128, 8])

        pS = [ctx.enter_context(nc.psum_tensor(f"pS{i}", [128, 1024], F32)) for i in range(2)]
        pT = [ctx.enter_context(nc.psum_tensor(f"pT{i}", [128, 512], F32)) for i in range(2)]
        pY = ctx.enter_context(nc.psum_tensor("pY", [128, 512], F32))
        pM = ctx.enter_context(nc.psum_tensor("pM", [128, 512], F32))

        ld_c = line("ld_c")
        ld_w = [line("ld_w0"), line("ld_w1")]
        ld_wo = [line("ld_wo0"), line("ld_wo1")]
        ld_q, ld_k, ld_v, ld_o, st = ([line(f"{n}{i}") for i in range(NT)] for n in (
            "ld_q", "ld_k", "ld_v", "ld_o", "st"))
        l_s, l_mx, l_ex, l_rc, l_sc, l_t, l_ph, l_pl, l_pv, l_yh, l_yl, l_c, l_acc = (line(n) for n in (
            "s", "mx", "ex", "rc", "sc", "t", "ph", "pl", "pv", "yh", "yl", "c", "acc"))
        l_m, l_qh, l_ql, l_r, l_rp, l_qs, l_qq, l_qp, l_k = (line(n) for n in (
            "m", "qh", "ql", "r", "rp", "qs", "qq", "qp", "k"))

        c_ld = None
        for dst, src in ((ident[:, :], A["ident"]), (maskf[:, :], A["mask"]),
                         (rope[:, :, :, :], A["rope"].rearrange("(n p) a d -> p n a d", p=128))):
            c_ld = put("scalar", [], lambda e, d=dst, s=src: e.dma_start(d, s), ld_c, 16, after=[c_ld], busy=60,
                       lag=3000, key=-9)
        q.key = -8
        a = put("gpsimd", [c_ld], lambda e: e.tensor_copy(identb[:, :], ident[:, :]), l_k, busy=500)
        a = put("gpsimd", [c_ld], lambda e: e.tensor_copy(identr[:, :], ident[:, :]), l_k, busy=500, after=[a])
        consts = put("gpsimd", [c_ld], lambda e: e.tensor_copy(maskb[:, :], maskf[:, :]), l_k, busy=500, after=[a])

        N = NB * NG * NT

        def where(n):
            return n // (NG * NT), n // NT % NG, n % NT

        wo = {}
        wb, lq, lk, lv, lo_, st_tok = {}, {}, {}, {}, {}, {}
        ex_tok, sc_tok, slots, slot_last, p_free = {}, {}, {}, {}, {}
        t_tok, pts, pt_lo, pt_pv = {}, {}, {}, {}
        y_lo, c_tok, acc_tok, a_last = {}, {}, {}, {}
        qdone, qpart, q_used, rope_done, qs_tok, tr_last = {}, {}, {}, {}, {}, {}
        state = {"m": None, "S": 0, "P": 0, "pt": 0, "pe_m": None}
        s_free = [None, None]

        def dma(waits, dst, src, ln, after=()):
            return put("sync", waits, lambda e: e.dma_start(dst, src), ln, 16, after=after,
                       busy=60 + dst.size() / 90, lag=2000)

        def load_w(gi, waits):
            wb[gi] = dma(waits, WB[:, gi % 2, 0:WO].bitcast(F32), wscr[gi % NG, :, 0:WO], ld_w[gi % 2])

        def load_wo(gi, waits):
            wo[gi] = dma(waits, WB[:, gi % 2, WO:].bitcast(F32), wscr[gi % NG, :, WO:], ld_wo[gi % 2])

        h_v = hscr.rearrange("t p (z a n) -> t p z a n", a=2, n=128)

        def load_h(t, waits, a, lines):
            i = t % NT
            c = slice(i * 128, (i + 1) * 128)
            first = dma(waits, H[:, a:4:2, c].bitcast(F32), h_v[t, :, 0:2, a, :], lines[i])
            return dma(waits, L[:, a:4:2, c].bitcast(F32), h_v[t, :, 2:4, a, :], lines[i], [first])

        def load_q(t, waits):
            lq[t] = load_h(t, waits, 0, ld_q)

        def load_k(t, waits):
            lk[t] = load_h(t, waits, 1, ld_k)

        def load_v(t, waits):
            lv[t] = dma(waits, V[:, t % NT, :].bitcast(F32), hscr[t, :, 1024:1280], ld_v[t % NT])

        def load_o(t, waits):
            lo_[t] = dma(waits, ACC[:, t % NT, :], oscr[t, :, :], ld_o[t % NT])

        def score(n, h):
            b, g, i = where(n)
            w = 128 * (i + 1)
            wide = max(256, w) if i != 4 else 768
            cuts = [(0, min(512, wide))] + ([(512, wide)] if wide > 512 else [])
            slot = state["S"] % 2
            S = pS[slot]
            state["S"] += 1
            ps = state["P"] % 8
            state["P"] += 1
            buf = (n // 2) % 2
            tq = slice((i % 2) * 128, (i % 2) * 128 + 128)
            qh, ql, qp = QH[:, buf, h, tq], QL[:, buf, h, tq], QP[:, buf, h, tq]
            tok = None
            for lo, hi in cuts:
                diag = lo <= 128 * i < hi

                def mul(e, lo=lo, hi=hi, diag=diag):
                    o = S[:, lo:hi]
                    e.matmul(o, qh, H[:, KA, lo:hi], start=True, stop=False)
                    e.matmul(o, qh, L[:, KA, lo:hi], start=False, stop=False)
                    e.matmul(o, ql, H[:, KA, lo:hi], start=False, stop=False)
                    e.matmul(o, qp, H[:, KB, lo:hi], start=False, stop=False)
                    m = e.matmul(o, qp, L[:, KB, lo:hi], start=False, stop=not diag)
                    if diag:
                        m = e.matmul(S[:, 128 * i:128 * i + 128], identb[:, :], maskb[:, :], start=False, stop=True)
                    return m
                waits = [lk[b * NT + t] for t in range(wide // 128)] + [consts, s_free[slot]]
                waits += list(qdone[n // 2][h // 2]) + [qpart[n // 2][i % 2]]
                tok = put("tensor", waits, mul, l_s, busy=mm(*[hi - lo] * 5, 128 if diag else 0), after=[tok, a_last.get(n)])
            a_last[n] = tok
            before = slot_last.get(ps)
            mx = put("vector", [tok, ex_tok.get(before)], lambda e: e.tensor_reduce(
                nm[:, ps:ps + 1], S[:, 0:w], AX_X, ALU.max, negate=True), l_mx, busy=dve(w))
            ex = put("scalar", [mx, p_free.get(ps), sc_tok.get(before)], lambda e: e.activation(
                P[:, ps, 0:w], S[:, 0:w], ACT.Exp, bias=nm[:, ps:ps + 1], accum_out=sm[:, ps:ps + 1]), l_ex,
                busy=act(w, 185))
            s_free[slot] = ex
            ex_tok[(n, h)] = ex
            slot_last[ps] = (n, h)
            r = put("vector", [ex], lambda e: e.reciprocal(rc[:, ps:ps + 1], sm[:, ps:ps + 1]), l_rc, busy=75)
            sc_tok[(n, h)] = put("vector", [r], lambda e: e.tensor_scalar(
                P[:, ps, 0:w], P[:, ps, 0:w], rc[:, ps:ps + 1], None, ALU.mult), l_sc, busy=dve2(w))
            slots[(n, h)] = ps

        def turn(n, j):
            k = state["pt"]
            state["pt"] += 1
            bank = pT[k % 2]
            pts[(n, j)] = k

            def tr(e):
                for h in range(4):
                    m = e.transpose(bank[:, h * 128:(h + 1) * 128], P[:, slots[(n, h)], j * 128:(j + 1) * 128],
                                    ident[:, :])
                return m
            t = put("tensor", [sc_tok[(n, h)] for h in range(4)] + [pt_lo.get(k - 2), c_ld], tr, l_t, busy=428,
                    after=[t_tok.get(k - 1)])
            t_tok[k] = t
            for h in range(4):
                p_free[slots[(n, h)]] = t
            hi = put("scalar", [t, pt_pv.get(k - 2)], lambda e: e.activation(
                PH[:, k % 2, :], bank[:, :], ACT.Copy), l_ph, busy=act(512))
            pt_lo[k] = put("vector", [hi], lambda e: e.tensor_tensor(
                PL[:, k % 2, :], bank[:, :], PH[:, k % 2, :], ALU.subtract), l_pl, busy=dve(512))

        def weigh(n, j):
            b, g, i = where(n)
            k = pts[(n, j)]
            s = k % 2

            def mul(e):
                e.matmul(pY[:, :], V[:, j, 0:128], PH[:, s, :], start=(j == 0), stop=False)
                e.matmul(pY[:, :], V[:, j, 128:256], PH[:, s, :], start=False, stop=False)
                return e.matmul(pY[:, :], V[:, j, 0:128], PL[:, s, :], start=False, stop=(j == i))
            pt_pv[k] = put("tensor", [pt_lo[k], lv[b * NT + j], y_lo.get(n - 1)], mul, l_pv, busy=640,
                           after=[pt_pv.get(k - 1)])
            if j == i:
                hi = put("scalar", [pt_pv[k], c_tok.get(n - 2)], lambda e: e.activation(
                    YH[:, n % 2, :], pY[:, :], ACT.Copy), l_yh, busy=act(512))
                y_lo[n] = put("vector", [hi], lambda e: e.tensor_tensor(
                    YL[:, n % 2, :], pY[:, :], YH[:, n % 2, :], ALU.subtract), l_yl, busy=dve(512))

        def combine(n):
            b, g, i = where(n)
            W = WB[:, (n // NT) % 2, :]
            t = b * NT + i
            tok = None
            for h in range(4):
                def mul(e, h=h):
                    yh, yl = YH[:, n % 2, h * 128:(h + 1) * 128], YL[:, n % 2, h * 128:(h + 1) * 128]
                    wh = W[:, WO + 512 * h:WO + 512 * h + 512]
                    wl = W[:, WO + 2048 + 512 * h:WO + 2560 + 512 * h]
                    e.matmul(pM[:, :], yh, wh, start=(h == 0), stop=False)
                    e.matmul(pM[:, :], yh, wl, start=False, stop=False)
                    return e.matmul(pM[:, :], yl, wh, start=False, stop=(h == 3))
                tok = put("tensor", [y_lo[n], state["m"], wo[n // NT]], mul, l_c, busy=640,
                          after=[tok, state["pe_m"]])
            c_tok[n] = state["pe_m"] = tok
            acc_tok[n] = state["m"] = put("vector", [tok, lo_[t], acc_tok.get(n - NT)], lambda e: e.tensor_tensor(
                ACC[:, i, :], pM[:, :], ACC[:, i, :], ALU.add), l_acc, busy=dve(512))
            if g == NG - 1:
                st_tok[t] = dma([acc_tok[n]], out[b, i * 128:(i + 1) * 128, :], ACC[:, i, :], st[i])
                if b + 1 < NB:
                    load_o(t + NT, [st_tok[t]])
            if i == NT - 1 and n // NT + 2 < NB * NG:
                load_w(n // NT + 2, [tok])
                load_wo(n // NT + 2, [tok])

        def up(pr, half):
            b, g, i = where(2 * pr)
            W = WB[:, (pr // 4) % 2, :]
            c = slice(i * 128, i * 128 + 256)
            t = b * NT + i
            tok = None
            for k in range(2):
                def mul(e, k=k):
                    h = 2 * half + k
                    o = pM[:, k * 256:(k + 1) * 256]
                    mh = W[:, WMA + 128 * h:WMA + 128 * h + 128]
                    ml = W[:, WMA + 512 + 128 * h:WMA + 640 + 128 * h]
                    mb = W[:, WMB + 128 * h:WMB + 128 * h + 128]
                    e.matmul(o, mh, H[:, QA, c], start=True, stop=False)
                    e.matmul(o, mh, L[:, QA, c], start=False, stop=False)
                    e.matmul(o, ml, H[:, QA, c], start=False, stop=False)
                    e.matmul(o, mb, H[:, QB, c], start=False, stop=False)
                    return e.matmul(o, mb, L[:, QB, c], start=False, stop=True)
                tok = put("tensor", [wb[pr // 4], lq[t], lq[t + 1], state["m"]], mul, l_m, busy=545,
                          after=[tok, state["pe_m"]])
            state["pe_m"] = tok
            src = pM[:, :].rearrange("p (h n) -> p h n", h=2)
            b2, h2 = pr % 2, slice(2 * half, 2 * half + 2)
            free = a_last.get(2 * pr - 3)
            hi = put("scalar", [tok, free], lambda e: e.activation(QH[:, b2, h2, :], src, ACT.Copy), l_qh,
                     busy=act(512))
            lo = put("vector", [hi, free], lambda e: e.tensor_tensor(
                QL[:, b2, h2, :], src, QH[:, b2, h2, :], ALU.subtract), l_ql, busy=dve(512))
            state["m"] = lo
            qdone.setdefault(pr, {})[half] = (hi, lo)
            q_used[pr] = tok

        def up_pe(pr):
            b, g, i = where(2 * pr)
            W = WB[:, (pr // 4) % 2, :]
            t = b * NT + i
            tok = None
            for k in range(2):
                def mul(e, k=k):
                    c = slice((i + k) * 128, (i + k + 1) * 128)
                    o = pM[:, k * 256:(k + 1) * 256]
                    wh, wl, ws = W[:, WQA:WQA + 256], W[:, WQA + 256:WQA + 512], W[:, WQB:WQB + 256]
                    e.matmul(o, H[:, QA, c], wh, start=True, stop=False)
                    e.matmul(o, H[:, QA, c], wl, start=False, stop=False)
                    e.matmul(o, L[:, QA, c], wh, start=False, stop=False)
                    e.matmul(o, H[:, QB, c], ws, start=False, stop=False)
                    return e.matmul(o, L[:, QB, c], ws, start=False, stop=True)
                tok = put("tensor", [wb[pr // 4], lq[t], lq[t + 1], state["m"]], mul, l_m, busy=545,
                          after=[tok, state["pe_m"]])
            state["pe_m"] = tok
            src = pM[:, :].rearrange("p (t h d) -> p t h d", t=2, h=4)

            def tab(a, lo, hi):
                return rope[:, i:i + 2, a, lo:hi].unsqueeze(2).to_broadcast([128, 2, 4, hi - lo])
            prev = rope_done.get(pr - 1)
            a = put("vector", [tok, c_ld, prev], lambda e: e.tensor_tensor(
                R1[:, :, :, :], src, tab(0, 0, 64), ALU.mult), l_r, busy=dve(512))
            a = put("vector", [tok, c_ld, prev], lambda e: e.tensor_tensor(
                R2[:, :, :, 0:32], src[:, :, :, 32:64], tab(1, 0, 32), ALU.mult), l_r, busy=dve(256), after=[a])
            a = put("vector", [tok, c_ld, prev], lambda e: e.tensor_tensor(
                R2[:, :, :, 32:64], src[:, :, :, 0:32], tab(1, 32, 64), ALU.mult), l_r, busy=dve(256), after=[a])
            state["m"] = a
            r = put("gpsimd", [a], lambda e: e.tensor_tensor(
                R1[:, :, :, :], R1[:, :, :, :], R2[:, :, :, :], ALU.add), l_rp, busy=1225)
            hi = put("scalar", [r, tr_last.get(pr - 1)], lambda e: e.activation(
                QS[:, :, :, 0, :], R1[:, :, :, :], ACT.Copy), l_qs, busy=act(512, 40))
            rope_done[pr] = qs_tok[pr] = put("gpsimd", [hi, tr_last.get(pr - 1)], lambda e: e.tensor_tensor(
                QS[:, :, :, 1, :], R1[:, :, :, :], QS[:, :, :, 0, :], ALU.subtract), l_rp, busy=1225)

        def turn_pe(pr, k):
            def tr(e):
                for h in range(4):
                    m = e.transpose(pM[:, h * 128:(h + 1) * 128].bitcast(F32R),
                                    QS[:, k, h, :, :].rearrange("p a d -> p (a d)"), identr[:, :])
                return m
            tok = put("tensor", [qs_tok[pr], consts, state["m"]], tr, l_qq, busy=240, after=[state["pe_m"]])
            tr_last[pr] = state["pe_m"] = tok
            ev = put("scalar", [tok, a_last.get(2 * pr - 3)], lambda e: e.activation(
                QP[:, pr % 2, :, k * 128:(k + 1) * 128], pM[:, :].rearrange("p (h n) -> p h n", h=4), ACT.Copy),
                l_qp, busy=act(512))
            state["m"] = ev
            qpart.setdefault(pr, {})[k] = ev

        q.key = -7
        load_q(0, [])
        load_q(1, [])
        load_w(0, [])
        for t in range(2):
            load_k(t, [])
            load_v(t, [])
        load_wo(0, [])
        load_o(0, [])
        load_o(1, [])
        for t in range(2, NT):
            load_q(t, [])
            load_k(t, [])
            load_v(t, [])
            load_o(t, [])
        load_w(1, [])
        load_wo(1, [])

        for n in range(-3, N + 1):
            b, g, i = where(n)
            q.key = n + 0.1
            if n % 2 and 0 <= n + 3 < N:
                up_pe((n + 3) // 2)
            if 0 <= n - 1 < N:
                q.key = n + 0.2
                combine(n - 1)
            if n % 2 and 0 <= n + 3 < N:
                q.key = n + 0.3
                up((n + 3) // 2, 0)
                q.key = n + 0.6
                up((n + 3) // 2, 1)
            if n % 2 == 0 and 0 <= n + 2 < N:
                q.key = n + 0.3
                turn_pe((n + 2) // 2, 0)
                turn_pe((n + 2) // 2, 1)
            if 0 <= n + 1 < N:
                for h in range(4):
                    q.key = n + 0.05 + 0.2 * h
                    score(n + 1, h)
            if 0 <= n < N:
                for j in range(i + 1):
                    q.key = n + 0.9 * j / (i + 1)
                    turn(n, j)
                    q.key = n + 0.9 * (j + 1) / (i + 1) - 0.5
                    weigh(n, j)
                q.key = n + 0.9
                if b + 1 < NB and g == NG - 1:
                    nxt = (b + 1) * NT
                    if i == NT - 4:
                        for t in range(0, NT - 2):
                            load_q(nxt + t, [q_used[n // 2 + 1] if t >= 6 else q_used[n // 2]])
                    if i == NT - 3:
                        for t in range(NT - 2, NT):
                            load_q(nxt + t, [q_used[(n + 3) // 2]])
                    if i == NT - 2:
                        for t in range(NT):
                            load_k(nxt + t, [a_last[n + 1]])
                    if i == NT - 1:
                        for t in range(NT):
                            load_v(nxt + t, [pt_pv[pts[(n, i)]]])
        q.key = 1e6
        for i in range(NT):
            put("sync", [st_tok[(NB - 1) * NT + i]], None)
        q.run(nc)


def build(nc, A, out):
    hscr = nc.dram_tensor("hscr", [NB * NT, 128, 1280], F32).ap()
    oscr = nc.dram_tensor("oscr", [NB * NT, 128, 512], F32).ap()
    wscr = nc.dram_tensor("wscr", [NG, 128, WBLOB], F32).ap()
    prepare(nc, A, hscr, oscr, wscr)
    attend(nc, A, hscr, oscr, wscr, out)


_INS = {"x": "L0_attn_x", "Wq_down": "L0_attn_Wq_down", "q_norm": "L0_attn_q_norm_w", "Wq_up": "L0_attn_Wq_up",
        "Wq_pe": "L0_attn_Wq_pe", "Wkv_down": "L0_attn_Wkv_down", "kv_norm": "L0_attn_kv_norm_w",
        "Wkv_up": "L0_attn_Wkv_up", "Wk_pe": "L0_attn_Wk_pe", "k_pe_norm": "L0_attn_k_pe_norm_w",
        "Wo": "L0_attn_Wo", "weight": "L0_ffn_weight", "rram": "L0_ffn_rram_variation"}


def constants():
    inv = np.float32(1.0) / np.power(np.float32(10000.0), np.arange(0, 64, 2, dtype=np.float32) / np.float32(64))
    ang = np.outer(np.arange(1024, dtype=np.float32), inv.astype(np.float32)).astype(np.float32)
    cos, sin = np.cos(ang), np.sin(ang)
    rope = np.stack([np.concatenate([cos, cos], 1), np.concatenate([-sin, sin], 1)], 1).astype(np.float32)
    k = np.arange(128)
    mask = np.where(k[None, :] > k[:, None], np.float32(-3.0e38), np.float32(0)).astype(np.float32)
    return {"ident": np.eye(128, dtype=np.float32), "rope": np.ascontiguousarray(rope), "mask": mask}


def kernel(**inputs):
    import concourse.bacc as _bacc
    from concourse import mybir as _mybir
    from concourse.bass_utils import run_bass_kernel_spmd as _run

    nc = _bacc.Bacc("TRN2", target_bir_lowering=False, num_devices=1)
    arrays, aps = {}, {}
    named = {k: np.ascontiguousarray(inputs[v]) for k, v in _INS.items()}
    named.update(constants())
    for k, a in named.items():
        arrays[f"in_{k}"] = a
        aps[k] = nc.dram_tensor(f"in_{k}", a.shape, _mybir.dt.from_np(a.dtype), kind="ExternalInput").ap()
    out = nc.dram_tensor("out_0", (4, 1024, 512), F32, kind="ExternalOutput").ap()
    build(nc, aps, out)
    r = _run(nc, [arrays], core_ids=[0])
    return r.results[0]["out_0"]
```

```python
from contextlib import ExitStack

import numpy as np

import concourse.bass as bass
from concourse import mybir

F32 = mybir.dt.float32
F32R = mybir.dt.float32r
BF16 = mybir.dt.bfloat16
ALU = mybir.AluOpType
ACT = mybir.ActivationFunctionType
AX_X = mybir.AxisListType.X

NB = 4
NT = 8
NG = 4
QA, KA, QB, KB = range(4)
WMA, WMB, WQA, WQB, WO = 0, 1024, 1536, 2048, 2304
WBLOB = 6400
BASE = 36
ORDER = (0, 7, 1, 6, 2, 5, 3, 4)
ORDER_LAST = (3, 4, 2, 5, 0, 7, 6, 1)
NLAST = 4
K_ST = -1
K_PE, K_C, K_U0, K_U1, K_T, K_S, K_CC, K_W, K_H = -0.1, -0.3, 0.3, 0.6, 0.7, -0.03, 6, 4, 30
SCALE = float(192) ** -0.5
LN_EPS = 1e-5
RMS_EPS = 1e-6


class Line:

    def __init__(self, ctx, nc, name):
        self.sem = ctx.enter_context(nc.semaphore(name))
        self.value = 0


class Task:

    def __init__(self, engine, waits, issue, line, step, after, busy, lag, key):
        self.engine, self.issue, self.line, self.step = engine, issue, line, step
        self.waits = [w for w in waits if w is not None]
        self.after = [w for w in after if w is not None]
        self.busy, self.lag, self.key = busy, lag, key
        self.token = None


class Queues:

    ENGINES = ("tensor", "vector", "scalar", "gpsimd", "sync")
    HOP = {"tensor": 182, "vector": 150, "scalar": 170, "gpsimd": 165, "sync": 100}
    TO_TENSOR = 60

    def __init__(self):
        self.tasks = []
        self.key = 0

    def put(self, engine, waits, issue, line=None, step=1, after=(), busy=100, lag=0, key=None):
        t = Task(engine, waits, issue, line, step, after, busy, lag,
                 (self.key if key is None else key, len(self.tasks)))
        self.tasks.append(t)
        return t

    def order(self):
        left, users = {}, {}
        for t in self.tasks:
            needs = set(t.waits) | set(t.after)
            left[t] = len(needs)
            for w in needs:
                users.setdefault(w, []).append(t)
        open_ = {e: [t for t in self.tasks if t.engine == e and not left[t]] for e in self.ENGINES}
        free = {e: 0.0 for e in self.ENGINES}
        when = {t: 0.0 for t in self.tasks}
        out = {e: [] for e in self.ENGINES}
        for _ in self.tasks:
            at, e = min((max(free[e], min(when[t] for t in open_[e])), e) for e in self.ENGINES if open_[e])
            t = min((t for t in open_[e] if when[t] <= at), key=lambda t: t.key)
            open_[e].remove(t)
            free[e] = at + t.busy
            out[e].append(t)
            if t.line is not None:
                t.line.value += t.step
                t.token = (t.line.sem, t.line.value)
            for u in users.get(t, ()):
                same = t.engine == u.engine and t not in u.waits
                when[u] = max(when[u], free[e] + (0 if same else t.lag + self.HOP[e] + (self.TO_TENSOR if u.engine == "tensor" else 0)))
                left[u] -= 1
                if not left[u]:
                    open_[u.engine].append(u)
        return out, max(free.values())

    def play(self, tasks, eng):
        met = {}
        for t in tasks:
            for w in t.waits:
                sem, value = w.token
                if met.get(id(sem), 0) < value:
                    eng.wait_ge(sem, value)
                    met[id(sem)] = value
            if t.issue is None:
                continue
            last = t.issue(eng)
            if t.line is not None:
                last.then_inc(t.line.sem, t.step)

    def run(self, nc):
        out, _ = self.order()
        with nc.Block() as block:
            @block.sync
            def _(eng):
                self.play(out["sync"], eng)

            @block.gpsimd
            def _(eng):
                self.play(out["gpsimd"], eng)

            @block.scalar
            def _(eng):
                self.play(out["scalar"], eng)

            @block.vector
            def _(eng):
                self.play(out["vector"], eng)

            @block.tensor
            def _(eng):
                self.play(out["tensor"], eng)


def dve(n):
    return 69 + 1.04 * n


def dve2(n):
    return 130 + 0.52 * n


def act(n, extra=0):
    return 52 + 0.832 * n + extra


def mm(*cols):
    return sum(n / 2.4 for n in cols)


class Memory:

    def __init__(self, ctx, nc):
        self.nc = nc
        start = at = (nc.sbuf_base + 31) // 32 * 32
        self.place = {}

        def own(name, shape, dt=F32):
            nonlocal at
            self.place[name] = at
            t = self.over(name, name, 0, shape, dt)
            n = 2 if dt == BF16 else 4
            for k in shape[1:]:
                n *= k
            at += n
            return t

        self.ident = own("ident", [128, 128])
        self.identr = own("identr", [128, 128], F32R)
        self.mask = own("mask", [128, 128])
        self.rope = own("rope", [128, NT, 2, 64])
        self.WB = own("WB", [128, 2, WBLOB], F32R)
        self.HL = own("HL", [128, 2, 4, NT * 128], F32R)
        self.H, self.L = self.HL[:, 0, :, :], self.HL[:, 1, :, :]
        self.V = own("V", [128, NT, 256], F32R)
        self.P = own("P", [128, 8, 1024])
        self.QH = own("QH", [128, 2, 4, 256], F32R)
        self.QL = own("QL", [128, 2, 4, 256], F32R)
        self.QP = own("QP", [128, 2, 4, 256], F32R)
        self.R1 = own("R1", [128, 2, 4, 64])
        self.R2 = own("R2", [128, 2, 4, 64])
        self.QS = own("QS", [128, 2, 4, 2, 64], F32R)
        self.PH = own("PH", [128, 2, 512], F32R)
        self.PL = own("PL", [128, 2, 512], F32R)
        self.ACC = own("ACC", [128, NT, 512])
        self.YH = own("YH", [128, 2, 512], F32R)
        self.YL = own("YL", [128, 2, 512], F32R)
        self.rest = own("rest", [128, 1792], F32R)
        ctx.enter_context(nc.sbuf_tensor("map", [128, (at - start) // 4], F32))
        self.banks = [ctx.enter_context(nc.psum_tensor(f"bank{i}", [128, 1024], F32)) for i in range(4)]

    def over(self, name, base, at, shape, dt=F32):
        return self.nc.alloc_sbuf_tensor_at(name, shape, dt, offset=self.place[base] + 4 * at)


def token_parts(t, H, L, V, h_v, v_v):
    c = slice(t % NT * 128, (t % NT + 1) * 128)
    out = []
    for a in range(2):
        out.append((H[:, a:4:2, c].bitcast(F32), h_v[t, :, 0:2, a, :]))
        out.append((L[:, a:4:2, c].bitcast(F32), h_v[t, :, 2:4, a, :]))
    out.append((V[:, t % NT, :].bitcast(F32), v_v[t, :, 1024:1280]))
    return out


def prepare(nc, ctx, q, A, sh, hscr, oscr, wscr):
    def sb(name, shape, dt=F32):
        return ctx.enter_context(nc.sbuf_tensor(name, shape, dt))

    def line(name):
        return Line(ctx, nc, "p_" + name)

    put = q.put

    over = sh.over
    wdh = over("wdh", "P", 0, [128, 4, 384], F32R)
    wdl = over("wdl", "P", 1536, [128, 4, 384], F32R)
    wfh = over("wfh", "P", 3072, [128, 4, 512], F32R)
    wfl = over("wfl", "P", 5120, [128, 4, 512], F32R)
    tmp = over("tmp", "P", 7168, [128, 768], F32R)
    pa = over("pa", "P", 7936, [128, 256])
    XH = over("XH", "QH", 0, [128, 2, 512], F32R)
    XL = over("XL", "QH", 1024, [128, 2, 512], F32R)
    XQ = over("XQ", "QL", 0, [128, 2, 512], F32R)
    XN = over("XN", "QL", 1024, [128, 2, 512])
    X = over("X", "QP", 0, [128, 8, 512])
    XG = over("XG", "PH", 0, [128, 2, 512], BF16)
    kv = over("kv", "PH", 512, [128, 2, 256])
    pbw = over("pbw", "PL", 0, [128, 256])
    KR = over("KR", "PL", 256, [128, 3, 3, 64])
    junk = over("junk", "PL", 832, [128, 192])
    CR = over("CR", "ACC", 0, [128, 8, 384])
    OP = over("OP", "ACC", 3072, [128, 2, 512])
    HT = over("HT", "YH", 0, [128, 3, 1280], F32R)
    fw = over("fw", "HL", 0, [128, 4, 512])
    fr = over("fr", "HL", 2048, [128, 4, 512])
    FT = over("FT", "V", 0, [128, 2, 512])
    wo = over("wo", "V", 0, [128, 4, 512])
    wd = over("wd", "HL", 4096, [128, 4, 384])
    ua = over("ua", "HL", 4096 + 1536, [128, 512])
    ub = over("ub", "HL", 4096 + 2048, [128, 512])
    tk = over("tk", "HL", 4096 + 2560, [128, 512])
    tq = over("tq", "HL", 4096 + 3072, [128, 1024])
    ident, rope, H, L, V, WB = sh.ident, sh.rope, sh.H, sh.L, sh.V, sh.WB
    nw = sb("nw", [128, 384])
    eps = sb("eps", [128, 2])
    ST = sb("ST", [128, 4, 6])
    MV = sb("MV", [128, 2, 4, 2])
    SM = sb("SM", [128, 2, 5, 4])
    NM = sb("NM", [128, 2, 4])
    SS = sb("SS", [128, 2, 12])
    RM = sb("RM", [128, 2, 5, 12])
    C = sb("C", [128, 3, 512])

    pX, pD, (pF, pC), pW = ([b[:, 0:512], b[:, 512:1024]] for b in sh.banks)

    l_sq = line("sq")
    ld_i = line("ld_i")
    ld_c = line("ld_c")
    ld_f = line("ld_f")
    ld_d = line("ld_d")
    ld_r = line("ld_r")
    l_fwp = line("fwp")
    ld_w = line("ld_w")
    ld_wo = line("ld_wo")
    st_w = [line("st_w0"), line("st_w1")]
    ld_x = [line(f"ld_x{i}") for i in range(8)]
    st_h = [line(f"st_h{i}") for i in range(3)]
    st_o = [line(f"st_o{i}") for i in range(8)]
    l_eps, l_nw, l_wdh, l_wdl, l_fw0, l_fw1, l_fw2, l_fw = (line(n) for n in (
        "eps", "nw", "wdh", "wdl", "fw0", "fw1", "fw2", "fw"))
    l_st, l_xn, l_xt, l_xh, l_xl, l_xq = (line(n) for n in ("st", "xn", "xt", "xh", "xl", "xq"))
    l_d, l_f, l_cr, l_o, l_ss, l_cn, l_kp, l_ct, l_hh, l_hl, l_vv = (
        line(n) for n in ("d", "f", "cr", "o", "ss", "cn", "kp", "ct", "hh", "hl", "vv"))
    l_k = line("k")
    l_wt, l_we, l_wm, l_wh, l_wl = (line(n) for n in ("wt", "we", "wm", "wh", "wl"))

    x_tok = {}

    def dma(waits, dst, src, ln, after=()):
        return put("sync", waits, lambda e: e.dma_start(dst, src), ln, 16, after=after,
                   busy=60 + dst.size() / 90, lag=2000)

    def load_x(t, waits):
        x_tok[t] = dma(waits, X[:, t % 8, :], A["x"][t // NT, (t % NT) * 128:(t % NT + 1) * 128, :],
                       ld_x[t % 8])

    q.key = -10
    id_ld = put("scalar", [], lambda e: e.dma_start(ident[:, :], A["ident"]), ld_i, 16, busy=60, lag=2500)
    for t in range(2):
        load_x(t, [])
    d_ld = None
    for lo, n, w in ((0, 192, "Wq_down"), (192, 128, "Wkv_down"), (320, 64, "Wk_pe")):
        d_ld = dma([], wd[:, :, lo:lo + n], A[w].rearrange("(c p) n -> p c n", p=128), ld_d, [d_ld])
    for t in range(2, 4):
        load_x(t, [])
    c_ld = None
    for dst, src in (
        (nw[:, 0:192], A["q_norm"].rearrange("(a n) -> a n", a=1).to_broadcast([128, 192])),
        (nw[:, 192:320], A["kv_norm"].rearrange("(a n) -> a n", a=1).to_broadcast([128, 128])),
        (nw[:, 320:384], A["k_pe_norm"].rearrange("(a n) -> a n", a=1).to_broadcast([128, 64])),
    ):
        c_ld = put("scalar", [], lambda e, d=dst, s=src: e.dma_start(d, s), ld_c, 16, after=[c_ld], busy=60,
                   lag=9000)
    f_ld = None
    for dst, w in ((fw, "weight"), (fr, "rram")):
        f_ld = dma([], dst[:, :, :], A[w].rearrange("(c p) n -> p c n", p=128), ld_f, [f_ld])
    r_ld = dma([], rope[:, :, :, :], A["rope"].rearrange("(n p) a d -> p n a d", p=128), ld_r)
    r_ld = dma([], sh.mask[:, :], A["mask"], ld_r, [r_ld])
    for t in range(4, 8):
        load_x(t, [])

    put("gpsimd", [], lambda e: e.memset(eps[:, 0:1], LN_EPS), l_eps)
    consts = put("gpsimd", [id_ld], lambda e: e.tensor_copy(sh.identr[:, :], ident[:, :]), l_k, busy=500)
    eps_t = put("gpsimd", [], lambda e: e.memset(eps[:, 1:2], RMS_EPS), l_eps)
    put("scalar", [eps_t], lambda e: e.activation(junk[:, 0:1], eps[:, 0:1], ACT.Sqrt), l_sq, busy=1500, key=-20)
    nwq = put("vector", [c_ld], lambda e: e.tensor_scalar(nw[:, 0:192], nw[:, 0:192], SCALE, None, ALU.mult),
              l_nw)

    wd_hi = put("scalar", [d_ld], lambda e: e.activation(wdh[:, :, :], wd[:, :, :], ACT.Copy), l_wdh,
                busy=act(1536))
    wd_lo = put("vector", [wd_hi], lambda e: e.tensor_tensor(wdl[:, :, :], wd[:, :, :], wdh[:, :, :],
                                                             ALU.subtract), l_wdl, busy=dve(1536))

    q.key = 0.5
    ternary = []
    for c in range(4):
        g = ternary[c - 2] if c >= 2 else None
        a = put("vector", [f_ld, g], lambda e, c=c: e.tensor_scalar(
            FT[:, c % 2, :], fw[:, c, :], -0.2, -0.6, ALU.is_lt, ALU.mult), l_fw, busy=dve2(512))
        b = put("vector", [f_ld], lambda e, c=c: e.tensor_scalar(
            fw[:, c, :], fw[:, c, :], 0.2, 0.6, ALU.is_gt, ALU.mult), l_fw, busy=dve2(512), after=[a])
        a = put("gpsimd", [a], lambda e, c=c: e.tensor_tensor(
            fr[:, c, :], fr[:, c, :], FT[:, c % 2, :], ALU.add), l_fwp, busy=1225)
        ternary.append(put("vector", [a, b], lambda e, c=c: e.tensor_tensor(
            fr[:, c, :], fr[:, c, :], fw[:, c, :], ALU.add), l_fw, busy=dve(512)))
    w_free = [None, None]
    w_turn = 0
    for c in range(4):
        bank = pW[w_turn % 2]

        def tr(e, c=c, bank=bank):
            for o in range(4):
                m = e.transpose(bank[:, o * 128:(o + 1) * 128], fr[:, o, c * 128:(c + 1) * 128], ident[:, :])
            return m
        t = put("tensor", ternary + [id_ld, w_free[w_turn % 2]], tr, l_fw1, busy=440)
        h = put("scalar", [t], lambda e, c=c, bank=bank: e.activation(
            wfh[:, c, :], bank[:, :], ACT.Copy, scale=-0.5), l_fw2, busy=act(512))
        f_done = w_free[w_turn % 2] = put("vector", [h], lambda e, c=c, bank=bank: e.scalar_tensor_tensor(
            out=wfl[:, c, :], in0=bank[:, :], scalar=-0.5, in1=wfh[:, c, :], op0=ALU.mult,
            op1=ALU.subtract), l_fw, busy=dve(560))
        w_turn += 1

    T = NB * NT
    rstd, xn, xq, xt, xh, xl, dmm, fmm, cr, od = ({} for _ in range(10))
    cn, kp, ct, hh, hl, vv, rms, ostore, hstore, sqd = ({} for _ in range(10))
    normed = {}
    bn, oe, cb = {}, {}, {}
    l_od = line("od")
    l_kbs, l_vhs, l_vvd = line("kbs"), line("vhs"), line("vvd")
    l_oe = line("oe")
    ld_h, ld_l = line("ld_h"), line("ld_l")
    h_v = hscr.rearrange("t p (z a n) -> t p z a n", a=2, n=128)

    def tile_parts(t):
        return token_parts(t, H, L, V, h_v, hscr)

    roots = []

    def newton(s, var, eps_c, add, busy, first, free):
        r = put("scalar", [first, eps_t, free], lambda e: e.activation(
            s[:, 0, :], var, ACT.Sqrt, bias=eps_c), l_sq, busy=200)
        roots.append(r)
        v = put("vector", [first, free], lambda e: e.tensor_scalar(s[:, 1, :], var, add, None, ALU.add), l_st,
                busy=busy)
        y = put("vector", [r], lambda e: e.reciprocal(s[:, 2, :], s[:, 0, :]), l_st, busy=busy)
        a = put("vector", [y], lambda e: e.tensor_tensor(s[:, 3, :], s[:, 2, :], s[:, 2, :], ALU.mult), l_st,
                busy=busy)
        a = put("vector", [a, v], lambda e: e.tensor_tensor(s[:, 3, :], s[:, 3, :], s[:, 1, :], ALU.mult), l_st,
                busy=busy)
        a = put("vector", [a], lambda e: e.tensor_scalar(s[:, 3, :], s[:, 3, :], -0.5, 1.5, ALU.mult, ALU.add),
                l_st, busy=busy)
        return put("vector", [a], lambda e: e.tensor_tensor(s[:, 4, :], s[:, 2, :], s[:, 3, :], ALU.mult), l_st,
                   busy=busy)

    def stats(quad, k0, k1):
        m, c = quad % 2, slice(k0, k1)
        for k in range(k0, k1):
            t = 4 * quad + k
            a = put("vector", [x_tok[t], bn.get(t - 4)], lambda e, t=t, k=k: e.bn_stats(
                ST[:, k, :], X[:, t % 8, :]), l_st, busy=600)
            bn[t] = put("vector", [a, xn.get(t - 8)], lambda e, k=k: e.bn_aggr(MV[:, m, k, :], ST[:, k, :]),
                        l_st, busy=80)
        tok = newton(SM[:, m, :, c], MV[:, m, c, 1], eps[:, 0:1], LN_EPS, 75, bn[4 * quad + k1 - 1],
                     xn.get(4 * quad - 5))
        tok = put("vector", [tok], lambda e: e.scalar_tensor_tensor(
            out=NM[:, m, c], in0=MV[:, m, c, 0], scalar=-1.0, in1=SM[:, m, 4, c], op0=ALU.mult, op1=ALU.mult),
            l_st, busy=75)
        for k in range(k0, k1):
            rstd[4 * quad + k] = tok

    def norm(t):
        m, k = (t // 4) % 2, t % 4
        xn[t] = put("scalar", [rstd[t], xt.get(t - 2)], lambda e: e.activation(
            XN[:, t % 2, :], X[:, t % 8, :], ACT.Identity, bias=NM[:, m, k:k + 1], scale=SM[:, m, 4, k:k + 1]),
            l_xn, busy=act(512, 235), after=[xn.get(t - 1)])

    def turn(t):
        bank = pX[t % 2]

        def tr(e):
            for c in range(4):
                m = e.transpose(bank[:, c * 128:(c + 1) * 128], XN[:, t % 2, c * 128:(c + 1) * 128], ident[:, :])
            return m
        xt[t] = put("tensor", [xn[t], id_ld, xq.get(t - 2), xl.get(t - 2)], tr, l_xt, busy=440)
        xh[t] = put("scalar", [xt[t], dmm.get(t - 2)], lambda e: e.activation(
            XH[:, t % 2, :], bank[:, :], ACT.Copy), l_xh, busy=act(512))
        xl[t] = put("vector", [xh[t], dmm.get(t - 2)], lambda e: e.tensor_tensor(
            XL[:, t % 2, :], bank[:, :], XH[:, t % 2, :], ALU.subtract), l_xl, busy=dve(512))
        g = put("vector", [xh[t]], lambda e: e.tensor_scalar(
            XG[:, t % 2, :], bank[:, :], 0.33, None, ALU.is_gt), l_xq, busy=dve(512))
        xq[t] = put("vector", [g, xh[t], fmm.get(t - 2)], lambda e: e.scalar_tensor_tensor(
            out=XQ[:, t % 2, :], in0=bank[:, :], scalar=-0.33, in1=XG[:, t % 2, :], op0=ALU.is_lt,
            op1=ALU.subtract), l_xq, busy=dve(512))

    def project(t):
        bd = pD[t % 2]

        def down(e):
            for c in range(4):
                xhc, xlc = XH[:, t % 2, c * 128:(c + 1) * 128], XL[:, t % 2, c * 128:(c + 1) * 128]
                e.matmul(bd[:, 0:384], xhc, wdh[:, c, :], start=(c == 0), stop=False)
                e.matmul(bd[:, 0:384], xhc, wdl[:, c, :], start=False, stop=False)
                m = e.matmul(bd[:, 0:384], xlc, wdh[:, c, :], start=False, stop=(c == 3))
            return m

        def ffn(e):
            for c in range(4):
                xc = XQ[:, t % 2, c * 128:(c + 1) * 128]
                e.matmul(pF[:, :], xc, wfh[:, c, :], start=(c == 0), stop=False)
                m = e.matmul(pF[:, :], xc, wfl[:, c, :], start=False, stop=(c == 3))
            return m
        dmm[t] = put("tensor", [xl[t], wd_lo, cr.get(t - 2)], down, l_d, busy=mm(*[384] * 12))
        fmm[t] = put("tensor", [xq[t], f_done, oe.get(t - 1)], ffn, l_f, busy=mm(*[512] * 8))
        cr[t] = put("scalar", [dmm[t], normed.get(t - 8)], lambda e: e.activation(
            CR[:, t % 8, :], bd[:, 0:384], ACT.Copy), l_cr, busy=act(384))
        if t >= T - NLAST:
            oe[t] = od[t] = put("vector", [fmm[t], bn[t], xn[t]], lambda e: e.tensor_tensor(
                X[:, t % 8, :], pF[:, :], X[:, t % 8, :], ALU.add), l_od, busy=dve(512))
            ostore[t] = dma([od[t]], oscr[t, :, :], X[:, t % 8, :], st_o[t % 8])
            return
        oe[t] = put("scalar", [fmm[t], od.get(t - 2)], lambda e: e.activation(
            OP[:, t % 2, :], pF[:, :], ACT.Copy), l_oe, busy=act(512))
        od[t] = put("gpsimd", [oe[t], bn[t], xn[t]], lambda e: e.tensor_tensor(
            X[:, t % 8, :], OP[:, t % 2, :], X[:, t % 8, :], ALU.add), l_o, busy=1225)
        ostore[t] = dma([od[t]], oscr[t, :, :], X[:, t % 8, :], st_o[t % 8])
        if t + 8 < T:
            load_x(t + 8, [ostore[t]])

    def squares(t):
        k, m = t % 4, (t // 4) % 2
        for j, (lo, hi) in enumerate(((0, 192), (192, 320), (320, 384))):
            sqd[t] = put("scalar", [cr[t], rms.get(t - 8), sqd.get(t, sqd.get(t - 1))],
                         lambda e, j=j, lo=lo, hi=hi: e.activation(
                junk[:, 0:hi - lo], CR[:, t % 8, lo:hi], ACT.Square, scale=float(hi - lo) ** -0.5,
                accum_out=SS[:, m, 3 * k + j:3 * k + j + 1]), l_ss, busy=act(hi - lo, 180))

    def rms_part(quad, k0, k1):
        m, c = quad % 2, slice(3 * k0, 3 * k1)
        tok = newton(RM[:, m, :, c], SS[:, m, c], eps[:, 1:2], RMS_EPS, 80, sqd[4 * quad + k1 - 1],
                     normed.get(4 * quad - 5))
        for k in range(k0, k1):
            rms[4 * quad + k] = tok

    def compress(t):
        m, k, i, sl = (t // 4) % 2, t % 4, t % NT, t % 3
        r = [RM[:, m, 4, 3 * k + j:3 * k + j + 1] for j in range(3)]
        free = [rms[t], nwq, ct.get(t - 3)]
        a = cn.get(t - 1)
        for dst, lo, hi, rr, more in (
            (C[:, sl, 0:128], 0, 128, r[0], []), (C[:, sl, 256:320], 128, 192, r[0], []),
            (C[:, sl, 128:256], 192, 320, r[1], [vv.get(t - 3)]),
            (KR[:, sl, 0, :], 320, 384, r[2], [kp.get(t - 3)]),
        ):
            a = put("vector", free + more, lambda e, dst=dst, lo=lo, hi=hi, rr=rr: e.scalar_tensor_tensor(
                out=dst, in0=CR[:, t % 8, lo:hi], scalar=rr, in1=nw[:, lo:hi], op0=ALU.mult, op1=ALU.mult),
                l_cn, busy=dve(hi - lo), after=[a])
        cn[t] = normed[t] = a
        if t >= T - NLAST:
            kb = put("scalar", [a, ct.get(t - 3)], lambda e: e.activation(
                C[:, sl, 320:384], C[:, sl, 256:320], ACT.Copy), l_kbs, busy=150)
            p = None
        else:
            p = kb = put("gpsimd", [a, ct.get(t - 3)], lambda e: e.tensor_copy(
                C[:, sl, 320:384], C[:, sl, 256:320]), l_kp, busy=350)
        cb[t] = kb
        for dst, s0, s1 in (
            (KR[:, sl, 1, :], KR[:, sl, 0, :], rope[:, i, 0, :]),
            (KR[:, sl, 2, 0:32], KR[:, sl, 0, 32:64], rope[:, i, 1, 0:32]),
            (KR[:, sl, 2, 32:64], KR[:, sl, 0, 0:32], rope[:, i, 1, 32:64]),
        ):
            p = put("gpsimd", [a, r_ld, kp.get(t - 3)], lambda e, dst=dst, s0=s0, s1=s1: e.tensor_tensor(
                dst, s0, s1, ALU.mult), l_kp, busy=250, after=[p])
        b = p
        for o in (384, 448):
            b = put("gpsimd", [p, ct.get(t - 3)], lambda e, o=o: e.tensor_tensor(
                C[:, sl, o:o + 64], KR[:, sl, 1, :], KR[:, sl, 2, :], ALU.add), l_kp, busy=280, after=[b])
        kp[t] = b
        if t >= T - NLAST:
            vh = put("scalar", [a, hstore.get(t - 3)], lambda e: e.activation(
                HT[:, sl, 1024:1152], C[:, sl, 128:256], ACT.Copy), l_vhs, busy=200)
        else:
            vh = put("gpsimd", [a, hstore.get(t - 3)], lambda e: e.tensor_copy(
                HT[:, sl, 1024:1152], C[:, sl, 128:256]), l_vv, busy=550)
        vv[t] = put("vector" if t >= T - NLAST else "gpsimd", [vh, hstore.get(t - 3)], lambda e: e.tensor_tensor(
            HT[:, sl, 1152:1280], C[:, sl, 128:256], HT[:, sl, 1024:1152], ALU.subtract),
            l_vvd if t >= T - NLAST else l_vv, busy=dve(128) if t >= T - NLAST else 430)

    def turn_c(t):
        sl = t % 3

        def tr(e):
            for c in range(4):
                m = e.transpose(pC[:, c * 128:(c + 1) * 128], C[:, sl, c * 128:(c + 1) * 128], ident[:, :])
            return m
        ct[t] = put("tensor", [cn[t], kp[t], cb[t], hl.get(t - 1), id_ld], tr, l_ct, busy=440)
        hh[t] = put("scalar", [ct[t], hstore.get(t - 3)], lambda e: e.activation(
            HT[:, sl, 0:512], pC[:, :], ACT.Copy), l_hh, busy=act(512))
        hl[t] = put("vector", [hh[t]], lambda e: e.tensor_tensor(
            HT[:, sl, 512:1024], pC[:, :], HT[:, sl, 0:512], ALU.subtract), l_hl, busy=dve(512))
        hstore[t] = dma([hl[t], vv[t]], hscr[t, :, :], HT[:, sl, :].bitcast(F32), st_h[sl])

    wo_v = A["Wo"].rearrange("(h v) n -> v h n", v=128)
    kv_v = A["Wkv_up"].rearrange("p (a n) -> p a n", a=2)
    wst = {"t": [], "m": None, "w": ternary[-1], "q": [], "p": None, "store": {}, "ld": None, "turn": w_turn}

    def weights(g):
        stores = wst["store"]
        c4, c2 = slice(512 * g, 512 * g + 512), slice(256 * g, 256 * g + 256)
        ldd = wst["ld"]
        for dst, src, w in ((kv[:, :, :], kv_v[:, :, c2], "t"), (ua[:, :], A["Wq_up"][0:128, c4], "t"),
                            (ub[0:64, :], A["Wq_up"][128:192, c4], "t"),
                            (ub[64:128, :], A["Wq_up"][128:192, c4], "t"),
                            (pa[:, :], A["Wq_pe"][0:128, c2], "q"), (pbw[0:64, :], A["Wq_pe"][128:192, c2], "q"),
                            (pbw[64:128, :], A["Wq_pe"][128:192, c2], "q")):
            ldd = dma(wst[w], dst, src, ld_w, [ldd])
        wst["ld"] = ldd
        wo_ld = dma([wst["w"]], wo[:, :, :], wo_v[:, 4 * g:4 * g + 4, :], ld_wo)
        store = stores.get(g + 2)
        blob = WB[:, g % 2, :]

        def bank():
            k = wst["turn"] % 2
            wst["turn"] += 1
            return pW[k], w_free[k], k

        def tr(srcs):
            pk, free, k = bank()

            def go(e):
                for j, src in enumerate(srcs):
                    m = e.transpose(pk[:, j * 128:(j + 1) * 128], src, ident[:, :])
                return m
            wst["p"] = put("tensor", [ldd, id_ld, free], go, l_wt, busy=440, after=[wst["p"]])
            return pk, wst["p"], k
        pk, t0, k = tr([ua[:, h * 128:(h + 1) * 128] for h in range(4)])
        e0 = w_free[k] = put("scalar", [t0, wst["m"]], lambda e, pk=pk: e.activation(
            tq[:, 0:512], pk[:, :], ACT.Copy), l_we, busy=act(512))
        pk, t1, k = tr([ub[:, h * 128:(h + 1) * 128] for h in range(4)])
        e1 = w_free[k] = put("scalar", [t1, wst["m"]], lambda e, pk=pk: e.activation(
            tq[:, 512:1024], pk[:, :], ACT.Copy), l_we, busy=act(512))
        pk, t2, k = tr([kv[:, a, h * 128:(h + 1) * 128] for a in range(2) for h in range(2)])
        e2 = w_free[k] = put("scalar", [t2, wst["m"], wst["w"]], lambda e, pk=pk: e.activation(
            tk[:, :], pk[:, :], ACT.Copy), l_we, busy=act(512))
        wst["t"] = [t2]

        def products(off):
            pk, free, k = bank()

            def go(e):
                for h in range(4):
                    m = e.matmul(pk[:, h * 128:(h + 1) * 128], tq[:, off + h * 128:off + (h + 1) * 128],
                                 tk[:, (h // 2) * 128:(h // 2 + 1) * 128], start=True, stop=True)
                return m
            wst["p"] = put("tensor", [e0, e1, e2, free], go, l_wm, busy=880, after=[wst["p"]])
            return pk, wst["p"], k

        def two_parts(pk, tok, k, hi, lo):
            a = put("scalar", [tok, store], lambda e: e.activation(hi, pk[:, :], ACT.Copy), l_wh,
                    busy=act(512))
            w_free[k] = put("vector", [a, store], lambda e: e.tensor_tensor(lo, pk[:, :], hi, ALU.subtract),
                            l_wl, busy=dve(512))
            return [a, w_free[k]]

        def stacked(src, n, at, off, tok, free):
            a = put("scalar", [tok, store], lambda e: e.activation(
                blob[0:64, at:at + n], src[0:64, :], ACT.Copy), l_wh, busy=act(n))
            b = put("scalar", [tok, free], lambda e: e.activation(
                tmp[64:128, off:off + n], src[64:128, :], ACT.Copy), l_wh, busy=act(n))
            c = put("vector", [a, b, store], lambda e: e.tensor_tensor(
                blob[64:128, at:at + n], src[64:128, :], tmp[64:128, off:off + n], ALU.subtract), l_wl,
                busy=dve(n))
            return [a, b, c]
        done = []
        pk, t3, k = products(0)
        done += two_parts(pk, t3, k, blob[:, WMA:WMA + 512], blob[:, WMA + 512:WMA + 1024])
        pk, t4, k = products(512)
        x = stacked(pk, 512, WMB, 0, t4, wst.get("tmp"))
        w_free[k] = x[-1]
        done += x
        wst["m"] = t4
        a = put("scalar", [ldd, store], lambda e: e.activation(blob[:, WQA:WQA + 256], pa[:, :], ACT.Copy), l_wh,
                busy=act(256))
        b = put("vector", [a, store], lambda e: e.tensor_tensor(
            blob[:, WQA + 256:WQA + 512], pa[:, :], blob[:, WQA:WQA + 256], ALU.subtract), l_wl, busy=dve(256))
        x = stacked(pbw, 256, WQB, 512, ldd, wst.get("tmp"))
        done += [a, b] + x
        wst["tmp"] = x[-1]
        wst["q"] = [b, x[-1]]
        for h in range(4):
            pk, free, k = bank()
            w = put("tensor", [e2, wo_ld, free], lambda e, h=h, pk=pk: e.matmul(
                pk[:, :], tk[:, 256 + (h // 2) * 128:384 + (h // 2) * 128], wo[:, h, :], start=True, stop=True),
                l_wm, busy=860, after=[wst["p"]])
            wst["p"] = w
            done += two_parts(pk, w, k, blob[:, WO + 512 * h:WO + 512 * h + 512],
                              blob[:, WO + 2048 + 512 * h:WO + 2560 + 512 * h])
        wst["w"] = w
        stores[g] = dma(done, wscr[g, :, :], blob.bitcast(F32), st_w[g % 2])
        wst["end"] = done + [w, wst["t"][0]]

    for quad in range(T // 4 + 1):
        if quad < T // 4:
            q.key = 4 * quad + K_ST
            for k0, k1 in ((0, 4),) if quad else ((0, 1), (1, 2), (2, 4)):
                stats(quad, k0, k1)
            for t in range(4 * quad, 4 * quad + 4):
                q.key = t
                norm(t)
                turn(t)
                project(t)
                squares(t)
        if 1 <= quad:
            q.key = 4 * quad
            for k0, k1 in ((0, 4),) if quad < T // 4 else ((0, 2), (2, 4)):
                rms_part(quad - 1, k0, k1)
            for t in range(4 * quad - 4, 4 * quad):
                q.key = t + K_CC
                compress(t)
                turn_c(t)
        if quad == 3:
            q.key = 20
            early_h = None
            for t in range(NT):
                for j in (0, 2):
                    early_h = dma([hstore[t], f_done], *tile_parts(t)[j], ld_h, [early_h])
        if 1 <= quad <= NG:
            q.key = 4 * quad + K_W
            weights(NG - quad)
        if quad == NG:
            q.key = K_H
            early_l = None
            for t in range(NT):
                for j in (1, 3, 4):
                    early_l = dma([hstore[t], wd_hi, wd_lo] + wst["end"], *tile_parts(t)[j], ld_l, [early_l])
    return {
        "banks": [dmm[T - 1], fmm[T - 1], xq[T - 1], xl[T - 1], cr[T - 1], oe[T - 1], early_h, early_l, consts] + w_free
        + wst["end"],
        "roots": roots,
        "early": [dmm[T - 1], fmm[T - 1], xt[T - 1], xq[T - 1], xl[T - 1], cr[T - 1], oe[T - 1], od[T - 1], sqd[T - 1], early_h, early_l, r_ld,
                  consts] + w_free + wst["end"],
        "late": [normed[T - 1], kp[T - 1], vv[T - 1], hl[T - 1], hstore[T - 3], hstore[T - 2], hstore[T - 1], ostore[T - 2],
                 ostore[T - 1]],
        "h": hstore, "o": [ostore[t] for t in range(T)], "w": wst["store"],
    }


def attend(nc, ctx, q, sh, prep, hscr, oscr, wscr, out):
    def line(name):
        return Line(ctx, nc, "a_" + name)

    early = prep["early"]
    gate = {e: q.put(e, prep["banks"] if e == "tensor" else early, None, busy=0, key=(BASE - 10)) for e in q.ENGINES}

    def put(engine, waits, issue, line=None, step=1, after=(), busy=100, lag=0, key=None):
        return q.put(engine, waits, issue, line, step, list(after) + [gate[engine]], busy, lag, key)

    nm, sm, rc = (ctx.enter_context(nc.sbuf_tensor(n, [128, 8], F32)) for n in ("nm", "sm", "rc"))
    ident, identr, mask, rope = sh.ident, sh.identr, sh.mask, sh.rope
    WB, H, L, V = sh.WB, sh.H, sh.L, sh.V
    ACC, P, PH, PL, YH, YL = sh.ACC, sh.P, sh.PH, sh.PL, sh.YH, sh.YL
    QH, QL, QP, QS, R1, R2 = sh.QH, sh.QL, sh.QP, sh.QS, sh.R1, sh.R2
    pS, pT = sh.banks[0:2], [sh.banks[3][:, 0:512], sh.banks[2][:, 0:512]]
    pY, pM = sh.banks[2][:, 512:1024], sh.banks[3][:, 512:1024]

    l_rv, l_tab = line("rv"), line("tab")
    put("scalar", prep["roots"], lambda e: e.activation(sm[:, 0:1], rope[:, 0, 0, 0:1], ACT.Exp), l_tab, busy=1400,
        key=BASE - 9)
    ld_w = [line("ld_w0"), line("ld_w1")]
    ld_wo = [line("ld_wo0"), line("ld_wo1")]
    ld_q, ld_k, ld_v, ld_o, st = ([line(f"{n}{i}") for i in range(NT)] for n in (
        "ld_q", "ld_k", "ld_v", "ld_o", "st"))
    l_s, l_mx, l_ex, l_rc, l_sc, l_t, l_ph, l_pl, l_pv, l_yh, l_yl, l_c, l_acc = (line(n) for n in (
        "s", "mx", "ex", "rc", "sc", "t", "ph", "pl", "pv", "yh", "yl", "c", "acc"))
    l_m, l_qh, l_ql, l_r, l_rp, l_qs, l_qq, l_qp = (line(n) for n in (
        "m", "qh", "ql", "r", "rp", "qs", "qq", "qp"))

    N = NB * NG * NT

    def where(n):
        i = (ORDER_LAST if n // NT == NB * NG - 1 else ORDER)[n % NT]
        return n // (NG * NT), n // NT % NG, i

    def pair(pr):
        return sorted(where(2 * pr + k)[2] for k in range(2))

    H4, L4 = (z[:, :, :].rearrange("p a (t n) -> p a t n", n=128) for z in (H, L))
    wo = {}
    wb, lq, lk, lv, lo_, st_tok = {}, {}, {}, {}, {}, {}
    ex_tok, sc_tok, slots, slot_last, p_free = {}, {}, {}, {}, {}
    t_tok, t_free, pts, pt_lo, pt_pv = {}, {}, {}, {}, {}
    y_lo, c_tok, acc_tok, a_last = {}, {}, {}, {}
    qdone, qpart, rope_done, qs_tok, tr_last = {}, {}, {}, {}, {}
    state = {"m": None, "S": 0, "P": 0, "pt": 0, "bank": 0, "pe_m": None}
    s_free = [None, None]

    def dma(waits, dst, src, ln, after=()):
        return put("sync", waits, lambda e: e.dma_start(dst, src), ln, 16, after=after,
                   busy=60 + dst.size() / 90, lag=2000)

    def load_w(gi, waits):
        wb[gi] = dma(waits + [prep["w"][gi % NG]], WB[:, gi % 2, 0:WO].bitcast(F32), wscr[gi % NG, :, 0:WO], ld_w[gi % 2])

    def load_wo(gi, waits):
        wo[gi] = dma(waits + [prep["w"][gi % NG]], WB[:, gi % 2, WO:].bitcast(F32), wscr[gi % NG, :, WO:], ld_wo[gi % 2])

    h_v = hscr.rearrange("t p (z a n) -> t p z a n", a=2, n=128)

    def load_h(t, waits, a, lines):
        parts = token_parts(t, H, L, V, h_v, hscr)
        waits = waits + [prep["h"][t]]
        first = dma(waits, *parts[2 * a], lines[t % NT])
        return dma(waits, *parts[2 * a + 1], lines[t % NT], [first])

    def load_q(t, waits):
        lq[t] = load_h(t, waits, 0, ld_q)

    def load_k(t, waits):
        lk[t] = load_h(t, waits, 1, ld_k)

    def load_v(t, waits):
        lv[t] = dma(waits + [prep["h"][t]], *token_parts(t, H, L, V, h_v, hscr)[4], ld_v[t % NT])

    def load_o(t, waits):
        lo_[t] = dma(waits + [prep["o"][t]], ACC[:, t % NT, :], oscr[t, :, :], ld_o[t % NT])

    def score(n, h):
        b, g, i = where(n)
        w = 128 * (i + 1)
        wide = max(256, w)
        off = 128 if i == 4 else 0
        cut = min(512 - off, wide)
        cuts = [(0, cut)] + ([(cut, wide)] if wide > cut else [])
        slot = state["S"] % 2
        S = pS[slot]
        state["S"] += 1
        ps = state["P"] % 8
        state["P"] += 1
        buf = (n // 2) % 2
        half = pair(n // 2).index(i)
        tq = slice(half * 128, half * 128 + 128)
        qh, ql, qp = QH[:, buf, h, tq], QL[:, buf, h, tq], QP[:, buf, h, tq]
        tok = None
        for lo, hi in cuts:

            def mul(e, lo=lo, hi=hi):
                o = S[:, off + lo:off + hi]
                e.matmul(o, qh, H[:, KA, lo:hi], start=True, stop=False)
                e.matmul(o, qh, L[:, KA, lo:hi], start=False, stop=False)
                e.matmul(o, ql, H[:, KA, lo:hi], start=False, stop=False)
                e.matmul(o, qp, H[:, KB, lo:hi], start=False, stop=False)
                return e.matmul(o, qp, L[:, KB, lo:hi], start=False, stop=True)

            def first(e):
                o = S[:, 0:256].rearrange("p (a n) -> p a n", a=2)
                e.matmul(o, qh, sh.HL[:, :, KA, 0:128], start=True, stop=False)
                e.matmul(o, ql, sh.HL[:, :, KA, 0:128], start=False, stop=False)
                return e.matmul(o, qp, sh.HL[:, :, KB, 0:128], start=False, stop=True)
            if i == 0:
                mul = first
            waits = [lk[b * NT + t] for t in range(i + 1)] + [s_free[slot]]
            waits += list(qdone[n // 2][h // 2]) + [qpart[n // 2][half]]
            tok = put("tensor", waits, mul, l_s, busy=mm(*[hi - lo] * (5 if i else 3)), after=[tok, a_last.get(n)])
        a_last[n] = tok
        before = slot_last.get(ps)
        src, free = S[:, off:off + w], [p_free.get(ps), sc_tok.get(before)]
        if i == 0:
            tok = put("vector", [tok] + free, lambda e: e.tensor_tensor(
                P[:, ps, 0:128], S[:, 128:256], mask[:, :], ALU.add), l_mx, busy=dve(128))
            tok = s_free[slot] = put("vector", [tok], lambda e: e.tensor_tensor(
                P[:, ps, 0:128], S[:, 0:128], P[:, ps, 0:128], ALU.add), l_mx, busy=dve(128))
            src = P[:, ps, 0:128]
        else:
            d = slice(off + 128 * i, off + 128 * i + 128)
            tok = put("vector", [tok], lambda e: e.tensor_tensor(S[:, d], S[:, d], mask[:, :], ALU.add), l_mx,
                      busy=dve(128))
        mx = put("vector", [tok, ex_tok.get(before)], lambda e: e.tensor_reduce(
            nm[:, ps:ps + 1], src, AX_X, ALU.max, negate=True), l_mx, busy=dve(w))
        ex = put("scalar", [mx] + free, lambda e: e.activation(
            P[:, ps, 0:w], src, ACT.Exp, bias=nm[:, ps:ps + 1], accum_out=sm[:, ps:ps + 1]), l_ex,
            busy=act(w, 185))
        if i:
            s_free[slot] = ex
        ex_tok[(n, h)] = ex
        slot_last[ps] = (n, h)
        r = put("vector", [ex], lambda e: e.reciprocal(rc[:, ps:ps + 1], sm[:, ps:ps + 1]), l_rc, busy=75)
        sc_tok[(n, h)] = put("vector", [r], lambda e: e.tensor_scalar(
            P[:, ps, 0:w], P[:, ps, 0:w], rc[:, ps:ps + 1], None, ALU.mult), l_sc, busy=dve2(w))
        slots[(n, h)] = ps

    def bank_t(waits, issue, line, busy):
        x = state["bank"]
        state["bank"] += 1
        t = t_tok[x] = put("tensor", waits + [t_free.get(x - 2)], lambda e: issue(e, pT[x % 2]), line, busy=busy,
                           after=[t_tok.get(x - 1)])
        return t, pT[x % 2], x

    def turn(n, j):
        k = state["pt"]
        state["pt"] += 1
        pts[(n, j)] = k

        def tr(e, bank):
            for h in range(4):
                m = e.transpose(bank[:, h * 128:(h + 1) * 128], P[:, slots[(n, h)], j * 128:(j + 1) * 128],
                                ident[:, :])
            return m
        t, bank, x = bank_t([sc_tok[(n, h)] for h in range(4)], tr, l_t, 428)
        for h in range(4):
            p_free[slots[(n, h)]] = t
        hi = put("scalar", [t, pt_pv.get(k - 2)], lambda e: e.activation(
            PH[:, k % 2, :], bank[:, :], ACT.Copy), l_ph, busy=act(512))
        pt_lo[k] = t_free[x] = put("vector", [hi] + (late if k < 2 else []), lambda e: e.tensor_tensor(
            PL[:, k % 2, :], bank[:, :], PH[:, k % 2, :], ALU.subtract), l_pl, busy=dve(512))

    def weigh(n, j):
        b, g, i = where(n)
        k = pts[(n, j)]
        s = k % 2
        y_free = [y_lo[n - 1]] if n else late

        def mul(e):
            e.matmul(pY[:, :], V[:, j, 0:128], PH[:, s, :], start=(j == 0), stop=False)
            e.matmul(pY[:, :], V[:, j, 128:256], PH[:, s, :], start=False, stop=False)
            return e.matmul(pY[:, :], V[:, j, 0:128], PL[:, s, :], start=False, stop=(j == i))
        pt_pv[k] = put("tensor", [pt_lo[k], lv[b * NT + j]] + y_free, mul, l_pv, busy=640,
                       after=[pt_pv.get(k - 1)])
        if j == i:
            hi = put("scalar", [pt_pv[k], c_tok.get(n - 2)], lambda e: e.activation(
                YH[:, n % 2, :], pY[:, :], ACT.Copy), l_yh, busy=act(512))
            y_lo[n] = put("vector", [hi], lambda e: e.tensor_tensor(
                YL[:, n % 2, :], pY[:, :], YH[:, n % 2, :], ALU.subtract), l_yl, busy=dve(512))

    def combine(n):
        b, g, i = where(n)
        W = WB[:, (n // NT) % 2, :]
        t = b * NT + i
        tok = None
        for h in range(4):
            def mul(e, h=h):
                yh, yl = YH[:, n % 2, h * 128:(h + 1) * 128], YL[:, n % 2, h * 128:(h + 1) * 128]
                wh = W[:, WO + 512 * h:WO + 512 * h + 512]
                wl = W[:, WO + 2048 + 512 * h:WO + 2560 + 512 * h]
                e.matmul(pM[:, :], yh, wh, start=(h == 0), stop=False)
                e.matmul(pM[:, :], yh, wl, start=False, stop=False)
                return e.matmul(pM[:, :], yl, wh, start=False, stop=(h == 3))
            tok = put("tensor", [y_lo[n], state["m"], wo[n // NT]], mul, l_c, busy=640,
                      after=[tok, state["pe_m"]])
        c_tok[n] = state["pe_m"] = tok
        acc_tok[t] = state["m"] = put("vector", [tok, lo_[t], acc_tok.get(t)], lambda e: e.tensor_tensor(
            ACC[:, i, :], pM[:, :], ACC[:, i, :], ALU.add), l_acc, busy=dve(512))
        if g == NG - 1:
            st_tok[t] = dma([acc_tok[t]], out[b, i * 128:(i + 1) * 128, :], ACC[:, i, :], st[i])
            if b + 1 < NB:
                load_o(t + NT, [st_tok[t]])
        if n % NT == NT - 1 and n // NT + 2 < NB * NG:
            load_w(n // NT + 2, [tok])
            load_wo(n // NT + 2, [tok])

    def up(pr, half):
        b, g, _ = where(2 * pr)
        i, i2 = pair(pr)
        both = slice(i, i2 + 1, i2 - i)
        W = WB[:, (pr // 4) % 2, :]
        tok = None
        for k in range(2):
            def mul(e, k=k):
                h = 2 * half + k
                o = pM[:, k * 256:(k + 1) * 256].rearrange("p (t n) -> p t n", t=2)
                mh = W[:, WMA + 128 * h:WMA + 128 * h + 128]
                ml = W[:, WMA + 512 + 128 * h:WMA + 640 + 128 * h]
                mb = W[:, WMB + 128 * h:WMB + 128 * h + 128]
                e.matmul(o, mh, H4[:, QA, both, :], start=True, stop=False)
                e.matmul(o, mh, L4[:, QA, both, :], start=False, stop=False)
                e.matmul(o, ml, H4[:, QA, both, :], start=False, stop=False)
                e.matmul(o, mb, H4[:, QB, both, :], start=False, stop=False)
                return e.matmul(o, mb, L4[:, QB, both, :], start=False, stop=True)
            tok = put("tensor", [wb[pr // 4], lq[b * NT + i], lq[b * NT + i2], state["m"]], mul, l_m, busy=545,
                      after=[tok, state["pe_m"]])
        state["pe_m"] = tok
        src = pM[:, :].rearrange("p (h n) -> p h n", h=2)
        b2, h2 = pr % 2, slice(2 * half, 2 * half + 2)
        free = a_last.get(2 * pr - 3)
        hi = put("scalar", [tok, free], lambda e: e.activation(QH[:, b2, h2, :], src, ACT.Copy), l_qh,
                 busy=act(512))
        lo = put("vector", [hi, free], lambda e: e.tensor_tensor(
            QL[:, b2, h2, :], src, QH[:, b2, h2, :], ALU.subtract), l_ql, busy=dve(512))
        state["m"] = lo
        qdone.setdefault(pr, {})[half] = (hi, lo)
        if half == 1 and g == NG - 1 and b + 1 < NB:
            for x in (i, i2):
                load_q((b + 1) * NT + x, [tok])

    def up_pe(pr):
        b, g, _ = where(2 * pr)
        i, i2 = pair(pr)
        both = slice(i, i2 + 1, i2 - i)
        W = WB[:, (pr // 4) % 2, :]
        tok = None
        for k in range(2):
            def mul(e, k=k):
                c = slice((i, i2)[k] * 128, ((i, i2)[k] + 1) * 128)
                o = pM[:, k * 256:(k + 1) * 256]
                wh, wl, ws = W[:, WQA:WQA + 256], W[:, WQA + 256:WQA + 512], W[:, WQB:WQB + 256]
                e.matmul(o, H[:, QA, c], wh, start=True, stop=False)
                e.matmul(o, H[:, QA, c], wl, start=False, stop=False)
                e.matmul(o, L[:, QA, c], wh, start=False, stop=False)
                e.matmul(o, H[:, QB, c], ws, start=False, stop=False)
                return e.matmul(o, L[:, QB, c], ws, start=False, stop=True)
            tok = put("tensor", [wb[pr // 4], lq[b * NT + i], lq[b * NT + i2], state["m"]], mul, l_m, busy=545,
                      after=[tok, state["pe_m"]])
        state["pe_m"] = tok
        src = pM[:, :].rearrange("p (t h d) -> p t h d", t=2, h=4)

        def tab(a, lo, hi):
            return rope[:, both, a, lo:hi].unsqueeze(2).to_broadcast([128, 2, 4, hi - lo])
        prev = [rope_done.get(pr - 1)] if pr else prep["o"][-4:]
        a = put("vector", [tok] + prev, lambda e: e.tensor_tensor(
            R1[:, :, :, :], src, tab(0, 0, 64), ALU.mult), l_r, busy=dve(512))
        a = put("vector", [tok] + prev, lambda e: e.tensor_tensor(
            R2[:, :, :, 0:32], src[:, :, :, 32:64], tab(1, 0, 32), ALU.mult), l_r, busy=dve(256), after=[a])
        a = put("vector", [tok] + prev, lambda e: e.tensor_tensor(
            R2[:, :, :, 32:64], src[:, :, :, 0:32], tab(1, 32, 64), ALU.mult), l_r, busy=dve(256), after=[a])
        state["m"] = a
        eng, ln, busy = ("gpsimd", l_rp, 1225) if pr else ("vector", l_rv, dve(512))
        r = put(eng, [a], lambda e: e.tensor_tensor(
            R1[:, :, :, :], R1[:, :, :, :], R2[:, :, :, :], ALU.add), ln, busy=busy)
        hi = put("scalar", [r, tr_last.get(pr - 1)], lambda e: e.activation(
            QS[:, :, :, 0, :], R1[:, :, :, :], ACT.Copy), l_qs, busy=act(512, 40))
        rope_done[pr] = qs_tok[pr] = put(eng, [hi, tr_last.get(pr - 1)], lambda e: e.tensor_tensor(
            QS[:, :, :, 1, :], R1[:, :, :, :], QS[:, :, :, 0, :], ALU.subtract), ln, busy=busy)

    def turn_pe(pr, k):
        def tr(e, bank):
            for h in range(4):
                m = e.transpose(bank[:, h * 128:(h + 1) * 128].bitcast(F32R),
                                QS[:, k, h, :, :].rearrange("p a d -> p (a d)"), identr[:, :])
            return m
        tok, bank, x = bank_t([qs_tok[pr]], tr, l_qq, 240)
        tr_last[pr] = tok
        ev = t_free[x] = put("scalar", [tok, a_last.get(2 * pr - 3)] + ([] if pr else prep["o"][-8:]),
                             lambda e: e.activation(QP[:, pr % 2, :, k * 128:(k + 1) * 128],
                                                    bank[:, :].rearrange("p (h n) -> p h n", h=4), ACT.Copy),
                             l_qp, busy=act(512))
        qpart.setdefault(pr, {})[k] = ev

    late = prep["late"]
    q.key = BASE - 7
    for t in range(NT):
        lq[t] = lk[t] = lv[t] = None
        load_o(t, late)
    for gi in range(2):
        wb[gi] = wo[gi] = None

    last_reader = [max(p for p in range(NT) if ORDER[p] >= t) for t in range(NT)]
    for n in range(-3, N + 1):
        b, g, i = where(n)
        q.key = BASE + n + K_PE
        if n % 2 and 0 <= n + 3 < N:
            up_pe((n + 3) // 2)
        if 0 <= n - 1 < N:
            q.key = BASE + n + K_C
            combine(n - 1)
        if n % 2 and 0 <= n + 3 < N:
            q.key = BASE + n + K_U0
            up((n + 3) // 2, 0)
            q.key = BASE + n + K_U1
            up((n + 3) // 2, 1)
        if n % 2 == 0 and 0 <= n + 2 < N:
            q.key = BASE + n + 0.3
            if not 0 <= n < N:
                turn_pe((n + 2) // 2, 0)
                turn_pe((n + 2) // 2, 1)
        if 0 <= n + 1 < N:
            for h in range(4):
                q.key = BASE + n + K_S + 0.2 * h
                score(n + 1, h)
        if 0 <= n < N:
            for j in range(i + 1):
                q.key = BASE + n + 0.9 * j / (i + 1)
                turn(n, j)
                if n % 2 == 0 and n + 2 < N and j == i:
                    q.key = BASE + n + K_T
                    turn_pe((n + 2) // 2, 0)
                    turn_pe((n + 2) // 2, 1)
                q.key = BASE + n + 0.9 * (j + 1) / (i + 1) - 0.5
                weigh(n, j)
            q.key = BASE + n + 0.9
            for m in (n, n + 1):
                b, g, i = where(m)
                if b + 1 < NB and g == NG - 1:
                    for t in range(NT):
                        if last_reader[t] == m % NT and m == n + 1:
                            load_k((b + 1) * NT + t, [a_last[m]])
                        if last_reader[t] == m % NT and m == n:
                            load_v((b + 1) * NT + t, [pt_pv[pts[(m, i)]]])
    q.key = 1e6
    for w in prep["w"].values():
        put("sync", [w], None)
    for i in range(NT):
        put("sync", [st_tok[(NB - 1) * NT + i]], None)


def build(nc, A, out):
    hscr = nc.dram_tensor("hscr", [NB * NT, 128, 1280], F32).ap()
    oscr = nc.dram_tensor("oscr", [NB * NT, 128, 512], F32).ap()
    wscr = nc.dram_tensor("wscr", [NG, 128, WBLOB], F32).ap()
    with ExitStack() as ctx:
        sh = Memory(ctx, nc)
        q = Queues()
        prep = prepare(nc, ctx, q, A, sh, hscr, oscr, wscr)
        attend(nc, ctx, q, sh, prep, hscr, oscr, wscr, out)
        q.run(nc)


_INS = {"x": "L0_attn_x", "Wq_down": "L0_attn_Wq_down", "q_norm": "L0_attn_q_norm_w", "Wq_up": "L0_attn_Wq_up",
        "Wq_pe": "L0_attn_Wq_pe", "Wkv_down": "L0_attn_Wkv_down", "kv_norm": "L0_attn_kv_norm_w",
        "Wkv_up": "L0_attn_Wkv_up", "Wk_pe": "L0_attn_Wk_pe", "k_pe_norm": "L0_attn_k_pe_norm_w",
        "Wo": "L0_attn_Wo", "weight": "L0_ffn_weight", "rram": "L0_ffn_rram_variation"}


def constants():
    inv = np.float32(1.0) / np.power(np.float32(10000.0), np.arange(0, 64, 2, dtype=np.float32) / np.float32(64))
    ang = np.outer(np.arange(1024, dtype=np.float32), inv.astype(np.float32)).astype(np.float32)
    cos, sin = np.cos(ang), np.sin(ang)
    rope = np.stack([np.concatenate([cos, cos], 1), np.concatenate([-sin, sin], 1)], 1).astype(np.float32)
    k = np.arange(128)
    mask = np.where(k[None, :] > k[:, None], np.float32(-3.0e38), np.float32(0)).astype(np.float32)
    return {"ident": np.eye(128, dtype=np.float32), "rope": np.ascontiguousarray(rope), "mask": mask}


def kernel(**inputs):
    import concourse.bacc as _bacc
    from concourse import mybir as _mybir
    from concourse.bass_utils import run_bass_kernel_spmd as _run

    nc = _bacc.Bacc("TRN2", target_bir_lowering=False, num_devices=1)
    arrays, aps = {}, {}
    named = {k: np.ascontiguousarray(inputs[v]) for k, v in _INS.items()}
    named.update(constants())
    for k, a in named.items():
        arrays[f"in_{k}"] = a
        aps[k] = nc.dram_tensor(f"in_{k}", a.shape, _mybir.dt.from_np(a.dtype), kind="ExternalInput").ap()
    out = nc.dram_tensor("out_0", (4, 1024, 512), F32, kind="ExternalOutput").ap()
    build(nc, aps, out)
    r = _run(nc, [arrays], core_ids=[0])
    return r.results[0]["out_0"]
```
